# Optimizing a Trainium2 kernel written in Bass

```python
import numpy as np
import jax
import jax.numpy as jnp

def _softmax(x, axis=-1):
    return jax.nn.softmax(x, axis=axis)

def _gelu(x):
    return jax.nn.gelu(x, approximate=True)

def _silu(x):
    return jax.nn.silu(x)

def _sigmoid(x):
    return jax.nn.sigmoid(x)

def _layernorm(x, axis=-1, eps=1e-05):
    m = jnp.mean(x, axis=axis, keepdims=True)
    v = jnp.var(x, axis=axis, keepdims=True)
    return (x - m) / jnp.sqrt(v + eps)

def _scatter_add(tgt, idx, src, axis=0):
    return tgt.at[idx].add(src)

def _segment_sum(src, seg, n):
    return jax.ops.segment_sum(src, seg, n)
kernel_name = 'mk_xattn_ffn_d1_seqx_r8_fbab2f'

def setup_inputs(seed: int=0):
    np.random.seed(seed)
    _w = jnp.asarray

    def _rec_inputs():
        import jax
        import jax.numpy as jnp
        _rk = jax.random.key(seed)
        x = -0.0002928 + 1 * jax.random.normal(jax.random.fold_in(_rk, 1), (4, 256, 256), jnp.float32)
        _lenS = 256 - jax.random.randint(jax.random.fold_in(_rk, 7), (4,), 0, max(1, 256 // 4) + 1, jnp.int32)
        _lenS2 = 256 - jax.random.randint(jax.random.fold_in(_rk, 8), (4,), 0, max(1, 256 // 4) + 1, jnp.int32)
        _ctx_2048P = jax.random.normal(jax.random.fold_in(_rk, 11), (4, 16, 256), jnp.float32)
        _ctx_2048c = jax.random.dirichlet(jax.random.fold_in(_rk, 511), 0.3 * jnp.ones((16,), jnp.float32), (4, 256))
        _ctx_2048t = jnp.einsum('bsk,bkd->bsd', _ctx_2048c, _ctx_2048P)
        _ctx_2048t = _ctx_2048t * jax.lax.rsqrt(jnp.mean(jnp.square(_ctx_2048t)) + 1e-12) * 0.953939
        ctx_2048 = -1.39393e-06 + 0.999914 * (_ctx_2048t + 0.3 * jax.random.normal(jax.random.fold_in(_rk, 611), (4, 256, 256), jnp.float32))
        return (x, ctx_2048)
    x, ctx_2048 = _rec_inputs()

    def _L0_xattn_setup():
        import jax, jax.numpy as jnp
        import numpy as np
        B, S, E, NH = (2, 128, 256, 16)
        DH = E // NH
        EPS = 1e-06

        def _mlstm_forward(q, k, v, Wi, bi, Wf, bf, ln_scale):
            b, s, e = q.shape
            nh = Wi.shape[1]
            dh = e // nh
            x = jnp.concatenate([q, k, v], axis=-1)
            ig = (x @ Wi + bi).transpose(0, 2, 1)[..., None]
            fg = (x @ Wf + bf).transpose(0, 2, 1)[..., None]
            split = lambda t: t.reshape(b, s, nh, dh).transpose(0, 2, 1, 3)
            qh, kh, vh = (split(q), split(k), split(v))
            log_f = jax.nn.log_sigmoid(fg)
            log_f_cum = jnp.concatenate([jnp.zeros((b, nh, 1, 1), q.dtype), jnp.cumsum(log_f, axis=2)], axis=2)
            fg_mat = log_f_cum - jnp.transpose(log_f_cum, (0, 1, 3, 2))
            ltr = jnp.tril(jnp.ones((s, s), dtype=bool))
            log_fg = jnp.where(ltr, fg_mat[:, :, 1:, 1:], -jnp.inf)
            log_D = log_fg + jnp.transpose(ig, (0, 1, 3, 2))
            max_log_D = jnp.max(log_D, axis=-1, keepdims=True)
            D = jnp.exp(log_D - max_log_D)
            qk = jnp.einsum('bhsd,bhtd->bhst', qh, kh) / jnp.sqrt(jnp.asarray(dh, q.dtype))
            C = qk * D
            normalizer = jnp.maximum(jnp.abs(C.sum(-1, keepdims=True)), jnp.exp(-max_log_D))
            Cn = C / (normalizer + EPS)
            h = jnp.einsum('bhst,bhtd->bhsd', Cn, vh)
            mu = h.mean(-1, keepdims=True)
            var = ((h - mu) ** 2).mean(-1, keepdims=True)
            hn = (h - mu) * jax.lax.rsqrt(var + EPS)
            hn = hn * ln_scale.reshape(1, nh, 1, dh)
            return hn.transpose(0, 2, 1, 3).reshape(b, s, e)
        key = jax.random.key(seed)
        ks = jax.random.split(key, 6)
        q = jax.random.normal(ks[0], (B, S, E), dtype=jnp.float32)
        k = jax.random.normal(ks[1], (B, S, E), dtype=jnp.float32)
        v = jax.random.normal(ks[2], (B, S, E), dtype=jnp.float32)
        Wi = jax.random.normal(ks[3], (3 * E, NH), dtype=jnp.float32) * 0.02
        bi = jax.random.normal(ks[4], (NH,), dtype=jnp.float32) * 0.1
        Wf = jax.random.normal(ks[5], (3 * E, NH), dtype=jnp.float32) * 0.02
        bf = jnp.linspace(3.0, 6.0, NH, dtype=jnp.float32)
        ln_scale = jnp.ones((E,), dtype=jnp.float32)
        return {'q': q, 'k': k, 'v': v, 'Wi': Wi, 'bi': bi, 'Wf': Wf, 'bf': bf, 'ln_scale': ln_scale}
    _L0_xattn_all = _L0_xattn_setup()
    _L0_xattn_in = {k: v for k, v in _L0_xattn_all.items() if k in ('Wi', 'bi', 'Wf', 'bf', 'ln_scale')}
    del _L0_xattn_all

    def _L0_ffn_setup():
        import jax, jax.numpy as jnp
        import numpy as np
        B, S, H = (1, 128, 256)
        E, K = (32, 4)
        F, FS = (176, 704)
        CAP = 32

        def silu(x):
            return x * jax.nn.sigmoid(x)
        key = jax.random.key(seed)
        ks = jax.random.split(key, 9)
        sc = 0.02
        return {'hidden_states': jax.random.normal(ks[0], (B, S, H), jnp.float32), 'Wr': jax.random.normal(ks[1], (H, E), jnp.float32) * sc, 'Wg': jax.random.normal(ks[2], (E, H, F), jnp.float32) * sc, 'Wu': jax.random.normal(ks[3], (E, H, F), jnp.float32) * sc, 'Wd': jax.random.normal(ks[4], (E, F, H), jnp.float32) * sc, 'Wsg': jax.random.normal(ks[5], (H, FS), jnp.float32) * sc, 'Wsu': jax.random.normal(ks[6], (H, FS), jnp.float32) * sc, 'Wsd': jax.random.normal(ks[7], (FS, H), jnp.float32) * sc, 'Wse': jax.random.normal(ks[8], (H, 1), jnp.float32) * sc}
    _L0_ffn_all = _L0_ffn_setup()
    _L0_ffn_in = {k: v for k, v in _L0_ffn_all.items() if k in ('Wr', 'Wg', 'Wu', 'Wd', 'Wsg', 'Wsu', 'Wsd', 'Wse')}
    del _L0_ffn_all
    return {'x': x, 'ctx_2048': ctx_2048, 'L0_xattn_Wi': _L0_xattn_in['Wi'], 'L0_xattn_bi': _L0_xattn_in['bi'], 'L0_xattn_Wf': _L0_xattn_in['Wf'], 'L0_xattn_bf': _L0_xattn_in['bf'], 'L0_xattn_ln_scale': _L0_xattn_in['ln_scale'], 'L0_ffn_Wr': _L0_ffn_in['Wr'], 'L0_ffn_Wg': _L0_ffn_in['Wg'], 'L0_ffn_Wu': _L0_ffn_in['Wu'], 'L0_ffn_Wd': _L0_ffn_in['Wd'], 'L0_ffn_Wsg': _L0_ffn_in['Wsg'], 'L0_ffn_Wsu': _L0_ffn_in['Wsu'], 'L0_ffn_Wsd': _L0_ffn_in['Wsd'], 'L0_ffn_Wse': _L0_ffn_in['Wse']}

def reference(x, ctx_2048, L0_xattn_Wi, L0_xattn_bi, L0_xattn_Wf, L0_xattn_bf, L0_xattn_ln_scale, L0_ffn_Wr, L0_ffn_Wg, L0_ffn_Wu, L0_ffn_Wd, L0_ffn_Wsg, L0_ffn_Wsu, L0_ffn_Wsd, L0_ffn_Wse):
    import jax
    import jax.numpy as jnp

    def _L0_xattn_ref(q, k, v, Wi, bi, Wf, bf, ln_scale):
        import jax, jax.numpy as jnp
        import numpy as np
        B, S, E, NH = (2, 128, 256, 16)
        DH = E // NH
        EPS = 1e-06

        def _mlstm_forward(q, k, v, Wi, bi, Wf, bf, ln_scale):
            b, s, e = q.shape
            nh = Wi.shape[1]
            dh = e // nh
            x = jnp.concatenate([q, k, v], axis=-1)
            ig = (x @ Wi + bi).transpose(0, 2, 1)[..., None]
            fg = (x @ Wf + bf).transpose(0, 2, 1)[..., None]
            split = lambda t: t.reshape(b, s, nh, dh).transpose(0, 2, 1, 3)
            qh, kh, vh = (split(q), split(k), split(v))
            log_f = jax.nn.log_sigmoid(fg)
            log_f_cum = jnp.concatenate([jnp.zeros((b, nh, 1, 1), q.dtype), jnp.cumsum(log_f, axis=2)], axis=2)
            fg_mat = log_f_cum - jnp.transpose(log_f_cum, (0, 1, 3, 2))
            ltr = jnp.tril(jnp.ones((s, s), dtype=bool))
            log_fg = jnp.where(ltr, fg_mat[:, :, 1:, 1:], -jnp.inf)
            log_D = log_fg + jnp.transpose(ig, (0, 1, 3, 2))
            max_log_D = jnp.max(log_D, axis=-1, keepdims=True)
            D = jnp.exp(log_D - max_log_D)
            qk = jnp.einsum('bhsd,bhtd->bhst', qh, kh) / jnp.sqrt(jnp.asarray(dh, q.dtype))
            C = qk * D
            normalizer = jnp.maximum(jnp.abs(C.sum(-1, keepdims=True)), jnp.exp(-max_log_D))
            Cn = C / (normalizer + EPS)
            h = jnp.einsum('bhst,bhtd->bhsd', Cn, vh)
            mu = h.mean(-1, keepdims=True)
            var = ((h - mu) ** 2).mean(-1, keepdims=True)
            hn = (h - mu) * jax.lax.rsqrt(var + EPS)
            hn = hn * ln_scale.reshape(1, nh, 1, dh)
            return hn.transpose(0, 2, 1, 3).reshape(b, s, e)
        return _mlstm_forward(q, k, v, Wi, bi, Wf, bf, ln_scale)

    def _L0_ffn_ref(hidden_states, Wr, Wg, Wu, Wd, Wsg, Wsu, Wsd, Wse):
        import jax, jax.numpy as jnp
        import numpy as np
        B, S, H = (1, 128, 256)
        E, K = (32, 4)
        F, FS = (176, 704)
        CAP = 32

        def silu(x):
            return x * jax.nn.sigmoid(x)
        b, s_len, h = hidden_states.shape
        x = hidden_states.reshape(-1, h)
        T = x.shape[0]
        probs = jax.nn.softmax(x @ Wr, axis=-1)
        topw, topi = jax.lax.top_k(probs, K)
        topw = topw / jnp.sum(topw, axis=-1, keepdims=True)
        shared = silu(x @ Wsg) * (x @ Wsu) @ Wsd
        shared = shared * jax.nn.sigmoid(x @ Wse)
        sel = topi.reshape(-1)
        w = topw.reshape(-1)
        tok = jnp.repeat(jnp.arange(T), K)
        oh = jax.nn.one_hot(sel, E, dtype=jnp.int32)
        pos = (jnp.cumsum(oh, axis=0) * oh).sum(-1) - 1
        valid = (pos < CAP).astype(x.dtype)
        posc = jnp.clip(pos, 0, CAP - 1)
        xe = jnp.zeros((E, CAP, h), x.dtype).at[sel, posc].add(x[tok] * valid[:, None])
        g = silu(jnp.einsum('ech,ehf->ecf', xe, Wg))
        u = jnp.einsum('ech,ehf->ecf', xe, Wu)
        ye = jnp.einsum('ecf,efh->ech', g * u, Wd)
        y_pair = ye[sel, posc] * (w * valid)[:, None]
        out = shared.at[tok].add(y_pair)
        return out.reshape(b, s_len, h)
    x = x + _L0_xattn_ref(_layernorm(x, axis=-1), ctx_2048, ctx_2048, L0_xattn_Wi, L0_xattn_bi, L0_xattn_Wf, L0_xattn_bf, L0_xattn_ln_scale)
    x = x + _L0_ffn_ref(_layernorm(x, axis=-1), L0_ffn_Wr, L0_ffn_Wg, L0_ffn_Wu, L0_ffn_Wd, L0_ffn_Wsg, L0_ffn_Wsu, L0_ffn_Wsd, L0_ffn_Wse)
    return x

_drawn_inputs = setup_inputs


def setup_inputs(seed=0):
    import zlib

    import numpy as np

    out = dict(_drawn_inputs(seed))
    spreads = {'L0_xattn_ln_scale': (1.0, 0.2)}
    factors = {'L0_xattn_bi': 64.0,
     'L0_xattn_Wf': 3.313,
     'L0_ffn_Wr': 8.0,
     'L0_ffn_Wg': 8.0,
     'L0_ffn_Wu': 8.0,
     'L0_ffn_Wd': 8.0,
     'L0_ffn_Wsg': 7.266,
     'L0_ffn_Wsu': 7.226,
     'L0_ffn_Wsd': 7.215,
     'L0_ffn_Wse': 8.0}
    for name, (base, spread) in spreads.items():
        noise = np.random.default_rng([zlib.crc32(name.encode()), seed]).standard_normal(out[name].shape)
        drawn = base * np.exp(spread * noise) if base else spread * noise
        out[name] = jnp.asarray(drawn.astype(out[name].dtype))
    for name, factor in factors.items():
        out[name] = (out[name] * factor).astype(out[name].dtype)
    return out
```

```python
import concourse.bass as bass
from concourse import mybir
from contextlib import ExitStack

ALU = mybir.AluOpType
ACT = mybir.ActivationFunctionType
AX = mybir.AxisListType
F32 = mybir.dt.float32
F32R = mybir.dt.float32r
BF16 = mybir.dt.bfloat16
U32 = mybir.dt.uint32
I32 = mybir.dt.int32

P = 128
NEG = -1.0e30


def xattn_moe_kernel(nc: bass.Bass, x, ctx, Wi, bi, Wf, bf, ln_scale, Wr, Wg, Wu, Wd, Wsg, Wsu, Wsd, Wse, out):
    B, S, H = x.shape
    NH = Wi.shape[1]
    DH = H // NH
    NE, _, F = Wg.shape
    FS = Wsg.shape[1]
    TOPK = 4
    CAP = 32
    TB = S // P
    NT = B * TB
    KC = H // P
    HC = NH // KC
    GH = 4
    NG = NH // GH
    UB = TB * NG
    NU = B * UB
    HP = 32
    FCH = [(c, min(P, FS - c)) for c in range(0, FS, P)]
    NF = len(FCH)
    EG = P // CAP
    NJ = NE // EG
    FK = F // 2
    RC = NE + 2
    XW = H + NE
    LAST = NU + 12
    assert (B, S, H, NH, NE, F) == (4, 256, 256, 16, 32, 176) and TB == KC == 2 and DH == 16

    rows = nc.dram_tensor("routed_rows", (NT * P, XW), F32, kind="Internal").ap()

    with ExitStack() as es:
        at = [16512]

        def place(name, shape, dt, where=None):
            size = 2 if dt == BF16 else 4
            for n in shape[1:]:
                size *= n
            size = -(-size // 32) * 32
            if where is None:
                where = at[0]
                at[0] += size
            assert where + size <= 229344, (name, where + size)
            return nc.alloc_sbuf_tensor_at(name, shape, dt, offset=where)

        def sem(name):
            return es.enter_context(nc.semaphore(name))

        x_sb = place("x_sb", [P, NT, H], F32)
        pick_at = at[0]
        pick = place("pick", [P, NT, CAP * NE], BF16)
        qn = place("qn", [P, NT, H], F32, pick_at)
        wu_hi_at = at[0]
        wu_hi = place("wu_hi", [P, KC, 2, FS], F32R)
        wu_lo = place("wu_lo", [P, KC, 2, FS], F32R)
        wd_hi = place("wd_hi", [P, NF, H], F32R)
        wd_lo = place("wd_lo", [P, NF, H], F32R)
        wr_raw = place("wr_raw", [P, KC, RC], F32)
        wr_hi = place("wr_hi", [P, KC, RC], F32R)
        wr_lo = place("wr_lo", [P, KC, RC], F32R)
        x2t_hi = place("x2t_hi", [P, 2, KC, S], F32R)
        x2t_lo = place("x2t_lo", [P, 2, KC, S], F32R)
        x2w = place("x2w", [P, 2, TB, XW], F32)
        th = place("th", [P, 2, S], F32)
        s1 = place("s1", [P, 2, S], F32)
        hf = place("hf", [P, 2, S], F32)
        h_hi = place("h_hi", [P, 3, S], F32R)
        h_lo = place("h_lo", [P, 3, S], F32R)
        ident = place("ident", [P, P], F32)
        head_rows = place("head_rows", [P, KC, HC], BF16)
        batch_heads = place("batch_heads", [P, B, KC, HC], F32)
        row_head = place("row_head", [P, 2, GH], F32)
        ident_b = place("ident_b", [P, P], BF16)
        before_b = place("before_b", [P, P], BF16)
        ones_b = place("ones_b", [P, P], BF16)
        slot_no = place("slot_no", [P, CAP], BF16)
        expert_no = place("expert_no", [P, NE], F32)
        row_no = place("row_no", [P, NT, 2], BF16)
        own_expert = place("own_expert", [P, NJ, EG], F32)
        mhalf = place("mhalf", [P, NH], F32)
        ln_bc = place("ln_bc", [P, H], F32)
        stats = place("stats", [P, NT, 6], F32)
        mv = place("mv", [P, NT, 2], F32)
        rstd = place("rstd", [P, NT], F32)
        lg = place("lg", [P, TB, RC], F32)
        m8 = place("m8", [P, TB, 8], F32)
        i8 = place("i8", [P, TB, 8], U32)
        i8f = place("i8f", [P, TB, 8], F32)
        eq4 = place("eq4", [P, NE, TOPK], F32)
        sel = place("sel", [P, TB, NE], F32)
        sel_b = place("sel_b", [P, TB, NE], BF16)
        nmax = place("nmax", [P, TB], F32)
        ex = place("ex", [P, TB, NE], F32)
        ssum = place("ssum", [P, TB], F32)
        rsum = place("rsum", [P, TB], F32)
        gate = place("gate", [P, NT], F32)
        sofar = place("sofar", [P, NE], F32)
        sofar_b = place("sofar_b", [P, TB, NE], BF16)
        vt = place("vt", [P, TB, NE], F32)
        vb = place("vb", [P, TB, NE], BF16)
        idxf = place("idxf", [P, NJ, 2], F32)
        idx = place("idx", [P, NJ], I32)
        w4 = place("w4", [P, NJ, EG], F32)
        wslot = place("wslot", [P, NJ], F32)
        slot0_at = at[0]
        stage_u = place("stage_u", [P, KC, 2, FS], F32)
        stage_d_at = at[0]
        at[0] = slot0_at + 4 * (EG * 2 * KC * F + EG * 2 * H)
        stage_d = place("stage_d", [P, NF, H], F32, stage_d_at)

        att_at = at[0]
        ctx_sb = place("ctx_sb", [P, NT, H], F32)
        qT = place("qT", [P, KC, B * S], F32)
        ctxT = place("ctxT", [P, KC, B * S], F32)
        qbd = place("qbd", [P, 2, GH, S], F32)
        vaug = place("vaug", [P, 2, TB, NH, HP], F32)
        arg_r = place("arg_r", [51, 2, HC, S], BF16)
        arg_l = place("arg_l", [51, B, S], BF16)
        dd = place("dd", [P, 2, GH, P], F32)
        cc = place("cc", [P, 2, GH, P], F32)
        hT = place("hT", [P, 2, NG, P], F32)
        state = place("state", [P, 2, HC, HP], F32)
        qr = place("qr", [P, 2, P], F32)
        wv = place("wv", [P, 2, HC, HP], F32)
        headsel = place("headsel", [P, B, KC, P], F32)
        wtnm = place("wtnm", [P, 3, P], F32)
        gw = place("gw", [P, 3 * KC, 2, 32], F32)
        bias = place("bias", [P, 2], F32)
        causal = place("causal", [P, P], BF16)
        blockmask = place("blockmask", [P, HC, HP], F32)
        head4 = place("head4", [P, GH], F32)
        vmean = place("vmean", [P, TB, NH], F32)
        ig = place("ig", [P, S], F32)
        g1 = place("g1", [P, S], F32)
        g2 = place("g2", [P, S], F32)
        cum = place("cum", [P, S], F32)
        aa = place("aa", [P, S], F32)
        mm_ = place("mm_", [P, S], F32)
        nm = place("nm", [P, S], F32)
        wfac = place("wfac", [P, P], F32)
        rfac = place("rfac", [P, P], F32)
        a_part = place("a_part", [P, 3, S], BF16)
        m_part = place("m_part", [P, 3, S], BF16)
        negA0 = place("negA0", [P, 1], F32)
        den = place("den", [P, 2, NH], F32)
        inv = place("inv", [P, 2, NH], F32)
        hv = place("hv", [P, 2, NH, DH], F32)
        sq = place("sq", [P, NH, DH], F32)
        ssq = place("ssq", [P, 2, NH], F32)
        rs = place("rs", [P, 2, NH], F32)
        yy = place("yy", [P, 2, H], F32)
        att_end = at[0]

        up_bytes, down_bytes = 4 * EG * 2 * KC * F, 4 * EG * 2 * H
        slots_at = [slot0_at] + [att_at + n * (up_bytes + down_bytes) for n in range(3)] + [wu_hi_at]
        NS = len(slots_at)
        we_up = [place(f"we_up{n}", [P, EG, 2, KC, F], F32, a) for n, a in enumerate(slots_at)]
        we_dn = [place(f"we_dn{n}", [P, EG, 2, H], F32, a + up_bytes) for n, a in enumerate(slots_at)]
        at[0] = att_at + 3 * (up_bytes + down_bytes)
        NX = 4
        back = place("back", [P, 2, NT * P], F32R)
        xe = place("xe", [P, NX, XW], F32)
        xeT = place("xeT", [P, 2, KC, P], F32)
        eth = place("eth", [P, F], F32)
        es1 = place("es1", [P, F], F32)
        eh = place("eh", [P, F], F32)
        ehT = place("ehT", [FK, 2, P], F32)
        y_hi = place("y_hi", [P, 2, H], F32R)
        y_lo = place("y_lo", [P, 2, H], F32R)
        assert at[0] <= 229344, at[0]

        bank = [es.enter_context(nc.psum_tensor(f"bank{n}", [P, 512], F32)) for n in range(8)]
        qk_ps, arg_ps, pv_ps, ht_ps, up_ps, down_ps, misc_ps = bank[0:2], bank[2], bank[3], bank[4], bank[5], bank[6], bank[7]
        acc_ps, eup_ps, back_ps, edn_ps = bank[0:4], bank[4], bank[5], bank[6]
        ht3 = ht_ps[:, :].rearrange("p (h e) -> p h e", e=HP)

        x_in = [sem(f"x_in{b}") for b in range(B)]
        ctx_in = [sem(f"ctx_in{b}") for b in range(B)]
        gw_in, bias_in, ln_in, wr_in, stage_in = map(sem, ("gw_in", "bias_in", "ln_in", "wr_in", "stage_in"))
        argl_in = sem("argl_in")
        argr_in = [sem(f"argr_in{c}") for c in range(KC)]
        slot_in = [sem(f"slot_in{n}") for n in range(NS)]
        rows_out = [sem(f"rows_out{b}") for b in range(B)]
        out_done = sem("out_done")
        xe_in = [sem(f"xe_in{n}") for n in range(NX)]
        names = ("dve_chain act_chain pool_chain pads_zero minus_ready vpads_ready ident_ready identb_ready rows_made heads_made selector_ready "
                 "masks_made routing_ready masks_ready ln1_stats ln1_rstd qn_ready "
                 "tposed t_evac gates_ready gates_ln_in gates_e gates_l a_ready fac_ready parts_ready fact_ready wtnm_ready gw_summed "
                 "vaug_ready wv_ready qbd_ready arg_ready d_ready qk_ready c_ready pv_done pv_evac ht_ready norm1 norm_rs "
                 "x_new ln2_stats ln2_rstd x2_ready st_ready state_ready x2t_ready x2hi_ready x2lo_ready logits_ready "
                 "lg_copied nmax_ready ex_ready sel_ready rw_ready excl_ready pick_ready idx_ready idx_added up_ready th_ready "
                 "h_ready hhi_ready hlo_ready downf_done base_ready wshared_ready wr_ready down_all idx_int "
                 "xet_ready xet_evac eup_ready eth_ready eh_ready eht_ready eht_evac edn_ready yhi_ready ylo_ready "
                 "back_ready back_evac comb_done acc_ready final_ready wslot_ready gate_th weight_hi").split()
        s = {n: sem(n) for n in names}
        block = es.enter_context(nc.Block())

        tail = FCH[-1][1]
        weight_parts = [(wr_raw[:, :, :], wr_hi[:, :, :], wr_lo[:, :, :])]
        weight_parts += [(stage_u[:, k, :, :], wu_hi[:, k, :, :], wu_lo[:, k, :, :]) for k in range(KC)]
        weight_parts += [(stage_d[:, 0:NF - 1, :], wd_hi[:, 0:NF - 1, :], wd_lo[:, 0:NF - 1, :]),
                         (stage_d[0:tail, NF - 1, :], wd_hi[0:tail, NF - 1, :], wd_lo[0:tail, NF - 1, :])]

        def unit(n):
            b, u = divmod(n, UB)
            i, g = divmod(u, NG)
            return b, i, g, g // (NG // KC), g % (NG // KC)

        def tok(b, i):
            return slice(b * S + i * P, b * S + (i + 1) * P)

        up_steps = {(b + 1) * UB + 5 + f + (2 if b == B - 2 and f >= NF // 2 else 0): (b, f) for b in range(B) for f in range(NF)}

        def ffn_at(n, lag):
            return up_steps.get(n - lag)

        def after_batch(n, u):
            b = (n - u) // UB - 1
            return b if (n - u) % UB == 0 and 0 <= b < B else None

        @block.sync
        def _(sp):
            def load_batch(b):
                sp.dma_start(x_sb[:, TB * b:TB * b + TB, :], x[b].rearrange("(i p) h -> p i h", p=P)).then_inc(x_in[b], 16)
                sp.dma_start(ctx_sb[:, TB * b:TB * b + TB, :], ctx[b].rearrange("(i p) h -> p i h", p=P)).then_inc(ctx_in[b], 16)

            load_batch(0)
            sp.wait_ge(s["pads_zero"], 3)
            with nc.allow_non_contiguous_dma(reason="rows of 16 gates"):
                sp.dma_start(gw[:, :, 0, 0:NH], Wi.rearrange("(k p) g -> p k g", p=P)).then_inc(gw_in, 16)
                sp.dma_start(gw[:, :, 1, 0:NH], Wf.rearrange("(k p) g -> p k g", p=P)).then_inc(gw_in, 16)
                for b in range(1, B):
                    load_batch(b)
                for b in range(B):
                    sp.dma_start(bias[32 * b:32 * b + NH, 0:1], bi.rearrange("(h a) -> h a", a=1)).then_inc(bias_in, 16)
                    sp.dma_start(bias[32 * b:32 * b + NH, 1:2], bf.rearrange("(h a) -> h a", a=1)).then_inc(bias_in, 16)
                sp.dma_start(wr_raw[:, :, 0:NE], Wr.rearrange("(k p) e -> p k e", p=P)).then_inc(wr_in, 16)
                sp.dma_start(wr_raw[:, :, NE:NE + 1], Wse.rearrange("(k p) e -> p k e", p=P)).then_inc(wr_in, 16)
            sp.dma_start(ln_bc[:, :], ln_scale.rearrange("(a h) -> a h", a=1).broadcast_to([P, H])).then_inc(ln_in, 16)
            sp.dma_start(stage_u[:, :, 0, :], Wsg.rearrange("(k p) f -> p k f", p=P)).then_inc(stage_in, 16)
            sp.dma_start(stage_u[:, :, 1, :], Wsu.rearrange("(k p) f -> p k f", p=P)).then_inc(stage_in, 16)
            sp.dma_start(stage_d[:, 0:NF - 1, :], Wsd[0:(NF - 1) * P, :].rearrange("(c p) h -> p c h", p=P)).then_inc(stage_in, 16)
            sp.dma_start(stage_d[0:FCH[-1][1], NF - 1, :], Wsd[(NF - 1) * P:FS, :]).then_inc(stage_in, 16)

            sp.wait_ge(s["minus_ready"], 1)
            sp.wait_ge(s["parts_ready"], 1)
            for part in range(3):
                for b in range(B):
                    sp.dma_start(arg_l[16 * part:16 * part + NH, b, :], a_part[32 * b:32 * b + NH, part, :]).then_inc(argl_in, 16)

            def load_arg_r(b, c):
                if b > 0:
                    sp.wait_ge(s["arg_ready"], UB * (b - 1) + NG + (NG // KC) * (c + 1))
                for part in range(3):
                    sp.dma_start(arg_r[48 + part:49 + part, c, :, :], m_part[32 * b + HC * c:32 * b + HC * c + HC, part, :]).then_inc(argr_in[c], 16)

            def load_slot(j):
                n = j % NS
                sp.dma_start(we_up[n][:, :, 0, :, :], Wg[EG * j:EG * j + EG].rearrange("e (p k) f -> p e k f", k=KC)).then_inc(slot_in[n], 16)
                sp.dma_start(we_up[n][:, :, 1, :, :], Wu[EG * j:EG * j + EG].rearrange("e (p k) f -> p e k f", k=KC)).then_inc(slot_in[n], 16)
                sp.dma_start(we_dn[n][0:FK, :, :, :], Wd[EG * j:EG * j + EG].rearrange("e (p k) h -> p e k h", k=2)).then_inc(slot_in[n], 16)

            sp.wait_ge(s["parts_ready"], 2)
            for c in range(KC):
                load_arg_r(0, c)
            sp.wait_ge(s["wshared_ready"], 4)
            load_slot(0)
            for b in range(1, B):
                for c in range(KC):
                    load_arg_r(b, c)
            sp.wait_ge(s["pv_done"], NU)
            sp.wait_ge(s["ht_ready"], NT)
            sp.wait_ge(s["norm1"], NT)
            sp.wait_ge(s["x_new"], NT)
            for j in range(1, 4):
                load_slot(j)
            sp.wait_ge(s["downf_done"], B * NF)
            load_slot(4)
            for j in range(NS, NJ):
                sp.wait_ge(s["edn_ready"], j - NS + 1)
                load_slot(j)
            for q in range(4):
                sp.wait_ge(s["final_ready"], q + 1)
                b = (TB * q) // TB
                sp.dma_start(out[b].rearrange("(i p) h -> p i h", p=P), x_sb[:, TB * q:TB * q + TB, :]).then_inc(out_done, 16)
            sp.wait_ge(out_done, 64)

        @block.gpsimd
        def _(pool):
            count = [0]

            def link(ins):
                count[0] += 1
                ins.then_inc(s["pool_chain"], 1)
                pool.wait_ge(s["pool_chain"], count[0])

            def band(view, op, base, pattern, mult, fill=1.0):
                return pool.affine_select(out=view, in_=view, compare_op=op, fill=fill, base=base, pattern=pattern, channel_multiplier=mult)

            link(pool.memset(head_rows[:, :, :], 0.0))
            for part in range(2):
                link(band(head_rows[:, :, :], ALU.not_equal, -16 * part, [[-HC, KC], [-1, HC]], 1))
            band(head_rows[:, :, :], ALU.not_equal, -32, [[-HC, KC], [-1, HC]], 1).then_inc(s["rows_made"], 1)
            link(pool.memset(ident[:, :], 0.0))
            band(ident[:, :], ALU.not_equal, 0, [[-1, P]], 1).then_inc(s["ident_ready"], 1)
            link(pool.memset(batch_heads[:, :, :, :], 0.0))
            band(batch_heads[:, :, :, :], ALU.not_equal, 0, [[-32, B], [-HC, KC], [-1, HC]], 1).then_inc(s["heads_made"], 1)
            link(pool.memset(row_head[:, :, :], 1.0))
            link(band(row_head[:, :, :], ALU.is_ge, 0, [[-DH * GH, 2], [-DH, GH]], 1, 0.0))
            link(band(row_head[:, :, :], ALU.is_ge, DH - 1, [[DH * GH, 2], [DH, GH]], -1, 0.0))
            pool.tensor_tensor(head4[:, :], row_head[:, 0, :], row_head[:, 1, :], ALU.add).then_inc(s["heads_made"], 1)
            link(pool.memset(causal[:, :], 0.0))
            band(causal[:, :], ALU.is_ge, 0, [[1, P]], -1, NEG).then_inc(s["masks_made"], 1)
            link(pool.memset(mhalf[:, :], -0.5))

            for b in range(B):
                pool.wait_ge(s["ln1_stats"], b + 1)
                r = slice(TB * b, TB * b + TB)
                link(pool.tensor_scalar(rstd[:, r], mv[:, r, 1], 1e-5, None, ALU.add))
                pool.tensor_tensor(rstd[:, r], rstd[:, r], mhalf[:, 0:TB], ALU.pow).then_inc(s["ln1_rstd"], 1)

            pool.wait_ge(gw_in, 32)
            pool.tensor_tensor(gw[:, KC:2 * KC, :, :], gw[:, KC:2 * KC, :, :], gw[:, 2 * KC:3 * KC, :, :], ALU.add).then_inc(s["gw_summed"], 1)


            def weigh_values(b, c):
                pool.wait_ge(s["vaug_ready"], b + 1)
                if b == 0 and c == 0:
                    pool.wait_ge(s["wtnm_ready"], 2)
                if b > 0:
                    pool.wait_ge(s["st_ready"], KC * (b - 1) + c + 1)
                w = wtnm[:, 0, 32 * b + HC * c:32 * b + HC * c + HC].unsqueeze(2).broadcast_to([P, HC, HP])
                pool.tensor_tensor(wv[:, c, :, :], vaug[:, b % 2, 0, HC * c:HC * c + HC, :], w, ALU.mult).then_inc(s["wv_ready"], 1)

            link(pool.memset(ones_b[:, :], 1.0))
            link(pool.memset(before_b[:, :], 1.0))
            link(band(before_b[:, :], ALU.is_gt, 0, [[1, P]], -1, 0.0))
            pool.iota(slot_no[:, :], [[1, CAP]], 0, 0, allow_small_or_imprecise_dtypes=True)
            pool.iota(expert_no[:, :], [[1, NE]], 0, 0, allow_small_or_imprecise_dtypes=True)
            pool.iota(row_no[:, :, 0], [[0, NT]], 0, 1, allow_small_or_imprecise_dtypes=True)
            pool.iota(row_no[:, :, 1], [[P, NT]], 0, 0, allow_small_or_imprecise_dtypes=True)
            link(pool.memset(own_expert[:, :, :], 1.0))
            link(band(own_expert[:, :, :], ALU.is_ge, 0, [[0, NJ], [-CAP, EG]], 1, 0.0))
            band(own_expert[:, :, :], ALU.is_ge, CAP - 1, [[0, NJ], [CAP, EG]], -1, 0.0).then_inc(s["routing_ready"], 1)
            for c in range(KC):
                weigh_values(0, c)
            for m, (raw, hi, lo) in enumerate(weight_parts):
                pool.wait_ge(s["weight_hi"], m + 1)
                pool.tensor_tensor(lo, raw, hi.bitcast(F32), ALU.subtract).then_inc(s["wr_ready" if m == 0 else "wshared_ready"], 1)

            for n in range(LAST + 1):
                k = (n - 5) // 4
                if n >= 5 and (n - 5) % 4 == 0 and k < NT:
                    pool.wait_ge(s["norm1"], k + 1)
                    pool.tensor_tensor(rs[:, k % 2, :], ssq[:, k % 2, :], mhalf[:, :], ALU.pow).then_inc(s["norm_rs"], 1)
                k = (n - 6) // 4
                if n >= 6 and (n - 6) % 4 == 0 and k < NT:
                    pool.wait_ge(s["ln2_stats"], k + 1)
                    link(pool.tensor_scalar(rstd[:, k:k + 1], mv[:, k, 1:2], 1e-5, None, ALU.add))
                    pool.tensor_tensor(rstd[:, k:k + 1], rstd[:, k:k + 1], mhalf[:, 0:1], ALU.pow).then_inc(s["ln2_rstd"], 1)
                b, u = divmod(n, UB)
                if b + 1 < B and u in (5, 7):
                    c = (u - 5) // 2
                    weigh_values(b + 1, c)
                bf_ = ffn_at(n, 1)
                if bf_:
                    b, f = bf_
                    m = NF * b + f
                    w = FCH[f][1]
                    pool.wait_ge(s["hhi_ready"], m + 1)
                    pool.tensor_tensor(h_lo[0:w, m % 3, :], hf[0:w, m % 2, :], h_hi[0:w, m % 3, :].bitcast(F32), ALU.subtract).then_inc(s["hlo_ready"], 1)
            pool.wait_ge(s["idx_int"], 1)
            for b in range(B):
                pool.wait_ge(rows_out[b], 16)
            for j in range(NJ):
                if j == 0:
                    pool.wait_ge(s["pv_done"], NU)
                    pool.wait_ge(s["ht_ready"], NT)
                    pool.wait_ge(s["norm1"], NT)
                    pool.wait_ge(s["x_new"], NT)
                if j >= NX:
                    pool.wait_ge(s["xet_ready"], j - NX + 1)
                    pool.wait_ge(s["wslot_ready"], j - NX + 1)
                pool.indirect_dma_start(xe[:, j % NX, :], None, rows[:, :], bass.IndirectOffsetOnAxis(ap=idx[:, j:j + 1], axis=0)).then_inc(xe_in[j % NX], 16)

        @block.scalar
        def _(act):
            count = [0]

            def link(ins):
                count[0] += 1
                ins.then_inc(s["act_chain"], 1)
                act.wait_ge(s["act_chain"], count[0])

            def build_qbd(m):
                b, c = divmod(m, KC)
                if m >= 2:
                    act.wait_ge(s["qk_ready"], UB * (b - 1) + NG + (NG // KC) * (c + 1))
                for h in range(GH):
                    ins = act.activation(qbd[:, c, h, :], qT[:, c, b * S:(b + 1) * S], ACT.Copy, scale=head4[:, h:h + 1])
                ins.then_inc(s["qbd_ready"], 1)

            def weight_hi(m):
                if m == 0:
                    act.wait_ge(wr_in, 32)
                elif m == 1:
                    act.wait_ge(stage_in, 64)
                raw, hi, lo = weight_parts[m]
                act.activation(hi, raw, ACT.Copy).then_inc(s["weight_hi"], 1)

            act.wait_ge(s["rows_made"], 1)
            act.activation(arg_r[0:3 * NH, :, :, :].rearrange("p c h s -> p (c h) s"),
                           head_rows[0:3 * NH, :, :].rearrange("p c h -> p (c h)").unsqueeze(2).broadcast_to([3 * NH, NH, S]), ACT.Copy).then_inc(s["selector_ready"], 1)
            for n in range(2 * B):
                b = n // 2
                act.wait_ge(s["tposed"], n + 1)
                dst = (ctxT if n % 2 == 0 else qT)[:, :, b * S:(b + 1) * S]
                act.activation(dst, bank[n % 4][:, :].rearrange("p (c t) -> p c t", c=KC), ACT.Copy).then_inc(s["t_evac"], 1)
            act.wait_ge(s["t_evac"], 2)
            act.wait_ge(s["heads_made"], 2)
            build_qbd(0)
            build_qbd(1)
            act.wait_ge(s["gates_ln_in"], 1)
            act.activation(nm[:, :], g1[:, :], ACT.Exp, scale=-1.0).then_inc(s["gates_e"], 1)
            act.wait_ge(s["gates_e"], 1)
            act.activation(nm[:, :], nm[:, :], ACT.Ln, bias=1.0).then_inc(s["gates_l"], 1)
            act.wait_ge(s["a_ready"], 1)
            act.activation(wfac[:, :], aa[:, 0:P], ACT.Exp, bias=negA0[:, :]).then_inc(s["fac_ready"], 1)
            act.activation(rfac[:, :], mm_[:, P:S], ACT.Exp, scale=-1.0, bias=mm_[:, P - 1:P]).then_inc(s["fac_ready"], 1)
            act.activation(nm[:, :], nm[:, :], ACT.Exp, scale=-1.0).then_inc(s["fac_ready"], 1)
            act.wait_ge(s["fact_ready"], 1)
            act.activation(wtnm[:, 1:3, :], ht_ps[:, P:3 * P].rearrange("p (a t) -> p a t", a=2), ACT.Copy, bias=1e-6).then_inc(s["wtnm_ready"], 1)
            act.activation(wtnm[:, 0, :], ht_ps[:, 0:P], ACT.Copy).then_inc(s["wtnm_ready"], 1)

            for n in range(LAST + 1):
                if n < NU:
                    act.wait_ge(s["arg_ready"], n + 1)
                    if n >= 2:
                        act.wait_ge(s["c_ready"], n - 1)
                    act.activation(dd[:, n % 2, :, :], arg_ps[:, :].rearrange("p (h t) -> p h t", h=GH), ACT.Exp).then_inc(s["d_ready"], 1)
                if n < len(weight_parts):
                    weight_hi(n)
                b, u = divmod(n, UB)
                if b + 1 < B and u in (5, 7):
                    if b == 0 and u == 5:
                        act.wait_ge(s["t_evac"], 2 * B)
                    build_qbd(KC * (b + 1) + (u - 5) // 2)
                bf_ = ffn_at(n, 1)
                if bf_:
                    b, f = bf_
                    m = NF * b + f
                    w = FCH[f][1]
                    act.wait_ge(s["h_ready"], m + 1)
                    if m >= 3:
                        act.wait_ge(s["downf_done"], m - 2)
                    act.activation(h_hi[0:w, m % 3, :], hf[0:w, m % 2, :], ACT.Copy).then_inc(s["hhi_ready"], 1)
                if n >= 4 and n % 4 == 0 and n // 4 - 1 < NT:
                    k = n // 4 - 1
                    act.wait_ge(s["pv_done"], 4 * k + 4)
                    if k >= 2:
                        act.wait_ge(s["ht_ready"], k - 1)
                    act.activation(hT[:, k % 2, :, :], pv_ps[:, :].rearrange("p (g t) -> p g t", g=NG), ACT.Copy).then_inc(s["pv_evac"], 1)
                b = after_batch(n, 4)
                if b is not None:
                    act.wait_ge(s["x2t_ready"], b + 1)
                    if b >= 2:
                        act.wait_ge(s["up_ready"], NF * (b - 1))
                        act.wait_ge(s["logits_ready"], b - 1)
                    act.activation(x2t_hi[:, b % 2, :, :], misc_ps[:, :].rearrange("p (c t) -> p c t", c=KC), ACT.Copy).then_inc(s["x2hi_ready"], 1)
                b = after_batch(n, 6)
                if b is not None:
                    act.wait_ge(s["nmax_ready"], b + 1)
                    for i in range(TB):
                        act.activation(ex[:, i, :], lg[:, i, 0:NE], ACT.Exp, bias=nmax[:, i:i + 1]).then_inc(s["ex_ready"], 1)
                    act.activation(gate[:, TB * b:TB * b + TB], lg[:, :, NE], ACT.Tanh, scale=0.5).then_inc(s["gate_th"], 1)
                b = after_batch(n, 7)
                if b is not None:
                    act.wait_ge(s["rw_ready"], b + 1)
                    act.dma_start(rows[b * S:(b + 1) * S, :].rearrange("(i p) w -> p i w", p=P), x2w[:, b % 2, :, :]).then_inc(rows_out[b], 16)
                bf_ = ffn_at(n, 0)
                if bf_:
                    b, f = bf_
                    m = NF * b + f
                    w = FCH[f][1]
                    act.wait_ge(s["up_ready"], m + 1)
                    if m >= 2:
                        act.wait_ge(s["h_ready"], m - 1)
                    act.activation(th[0:w, m % 2, :], up_ps[0:w, 0:S], ACT.Tanh, scale=0.5).then_inc(s["th_ready"], 1)
            for j in range(-1, NJ):
                if j + 1 < NJ:
                    act.wait_ge(s["xet_ready"], j + 2)
                    act.activation(xeT[:, (j + 1) % 2, :, :], misc_ps[:, 0:KC * P].rearrange("p (c t) -> p c t", c=KC), ACT.Copy).then_inc(s["xet_evac"], 1)
                    act.wait_ge(s["eup_ready"], j + 2)
                    if j >= 0:
                        act.wait_ge(s["eh_ready"], j + 1)
                    act.activation(eth[:, :], eup_ps[:, 0:F], ACT.Tanh, scale=0.5).then_inc(s["eth_ready"], 1)
                    act.wait_ge(s["back_ready"], j + 2)
                    if j >= 1:
                        act.wait_ge(s["comb_done"], j)
                    act.activation(back[:, (j + 1) % 2, :], back_ps[:, :].bitcast(BF16), ACT.Copy).then_inc(s["back_evac"], 1)
                    act.wait_ge(s["edn_ready"], j + 2)
                    act.wait_ge(s["wslot_ready"], j + 2)
                    if j >= 1:
                        act.wait_ge(s["comb_done"], j)
                    act.activation(y_hi[:, (j + 1) % 2, :], edn_ps[:, 0:H], ACT.Copy, scale=wslot[:, j + 1:j + 2]).then_inc(s["yhi_ready"], 1)

        @block.tensor
        def _(pe):
            pe.wait_ge(s["ident_ready"], 1)
            for n in range(2 * B):
                b = n // 2
                if n % 2 == 0:
                    pe.wait_ge(ctx_in[b], 16)
                else:
                    pe.wait_ge(s["qn_ready"], b + 1)
                if n >= 4:
                    pe.wait_ge(s["t_evac"], n - 3)
                src = ctx_sb if n % 2 == 0 else qn
                for c in range(KC):
                    for i in range(TB):
                        last = pe.transpose(bank[n % 4][:, (TB * c + i) * P:(TB * c + i + 1) * P], src[:, TB * b + i, c * P:(c + 1) * P], ident[:, :])
                last.then_inc(s["tposed"], 1)
            pe.wait_ge(s["gw_summed"], 1)
            for b in range(B):
                pe.wait_ge(s["t_evac"], 2 * b + 2)
                for gi in range(2):
                    for k in range(2 * KC):
                        src = qT if k < KC else ctxT
                        last = pe.matmul(misc_ps[32 * b:32 * b + 32, gi * S:(gi + 1) * S], gw[:, k, gi, :], src[:, k % KC, b * S:(b + 1) * S],
                                         start=(k == 0), stop=(k == 2 * KC - 1))
            last.then_inc(s["gates_ready"], 1)
            pe.wait_ge(s["fac_ready"], 3)
            for a, src in enumerate((wfac[:, :], nm[:, 0:P], nm[:, P:S])):
                last = pe.transpose(ht_ps[:, a * P:(a + 1) * P], src, ident[:, :])
            last.then_inc(s["fact_ready"], 1)
            pe.wait_ge(argl_in, 16 * 3 * B)
            pe.wait_ge(s["selector_ready"], 1)
            pe.wait_ge(s["masks_made"], 1)
            pe.wait_ge(s["identb_ready"], 1)
            pe.wait_ge(s["vpads_ready"], 1)

            def values(n):
                b, i, g, c, r = unit(n)
                pe.wait_ge(s["c_ready"], n + 1)
                if g == 0 and n > 0:
                    pe.wait_ge(s["pv_evac"], n // 4)
                if g == 0:
                    pe.wait_ge(s["vaug_ready"], b + 1)
                o = pv_ps[:, g * P:(g + 1) * P]
                if i == 1:
                    pe.wait_ge(s["state_ready"], KC * b + c + 1)
                    pe.matmul(o, state[:, c, GH * r:GH * r + GH, :].rearrange("p h e -> p (h e)"), qr[:, c, :], start=True, stop=False, skip_group_check=True)
                for h in range(GH):
                    last = pe.matmul(o[32 * h:32 * h + 32, :], vaug[:, b % 2, i, GH * g + h, :], cc[:, n % 2, h, :],
                                     start=(i == 0), stop=True, skip_group_check=True)
                last.then_inc(s["pv_done"], 1)

            for n in range(LAST + 1):
                if n < NU:
                    b, i, g, c, r = unit(n)
                    if i == 0 and r == 0:
                        pe.wait_ge(argr_in[c], 48 * (b + 1))
                    if n >= 1:
                        pe.wait_ge(s["d_ready"], n)
                    if n == 0:
                        pe.wait_ge(s["t_evac"], 2 * B)
                    pe.matmul(arg_ps[:, :], arg_l[:, b, i * P:(i + 1) * P], arg_r[:, c, GH * r:GH * r + GH, i * P:(i + 1) * P], start=True, stop=False)
                    pe.matmul(arg_ps[:, :], ident_b[:, :], causal[:, :].unsqueeze(1).broadcast_to([P, GH, P]), start=False, stop=True).then_inc(s["arg_ready"], 1)
                    if i == 0 and r == 0:
                        pe.wait_ge(s["qbd_ready"], KC * b + c + 1)
                    if n >= 2:
                        pe.wait_ge(s["c_ready"], n - 1)
                    pe.matmul(qk_ps[n % 2][:, :], ctxT[64 * r:64 * r + 64, c, tok(b, i)], qbd[64 * r:64 * r + 64, c, :, i * P:(i + 1) * P],
                              start=True, stop=True).then_inc(s["qk_ready"], 1)
                if 1 <= n <= NU:
                    values(n - 1)
                if n >= 5 and (n - 5) % 4 == 0 and (n - 5) // 4 < NT:
                    k = (n - 5) // 4
                    pe.wait_ge(s["pv_evac"], k + 1)
                    if k >= 1:
                        pe.wait_ge(s["norm1"], k)
                    for g in range(NG):
                        last = pe.transpose(ht_ps[:, g * P:(g + 1) * P], hT[:, k % 2, g, :], ident[:, :])
                    last.then_inc(s["ht_ready"], 1)
                b, u = divmod(n, UB)
                if b < B and u in (3, 4):
                    c = u - 3
                    pe.wait_ge(s["wv_ready"], KC * b + c + 1)
                    if b == 0 and c == 0:
                        pe.wait_ge(s["masks_ready"], 1)
                    if b > 0 or c > 0:
                        pe.wait_ge(s["state_ready"], KC * b + c)
                    if b >= 2:
                        pe.wait_ge(s["h_ready"], NF * (b - 1))
                    pe.matmul(up_ps[:, 0:HC * HP], ctx_sb[:, TB * b, c * P:(c + 1) * P], wv[:, c, :, :].rearrange("p h e -> p (h e)"), start=True, stop=True)
                    pe.matmul(up_ps[:, HC * HP:HC * HP + P], headsel[:, b, c, :], rfac[:, :], start=True, stop=True, skip_group_check=True).then_inc(s["st_ready"], 1)
                b = after_batch(n, 4)
                if b is not None:
                    pe.wait_ge(s["x2_ready"], TB * (b + 1))
                    if b == 0:
                        pe.wait_ge(s["a_ready"], 1)
                    else:
                        pe.wait_ge(s["idx_added"], b)
                    for c in range(KC):
                        for i in range(TB):
                            last = pe.transpose(misc_ps[:, (TB * c + i) * P:(TB * c + i + 1) * P], x2w[:, b % 2, i, c * P:(c + 1) * P], ident[:, :])
                    last.then_inc(s["x2t_ready"], 1)
                b = after_batch(n, 5)
                if b is not None:
                    pe.wait_ge(s["x2lo_ready"], b + 1)
                    if b == 0:
                        pe.wait_ge(s["wr_ready"], 1)
                    for i in range(TB):
                        for k in range(KC):
                            for m, (xs, ws) in enumerate(((x2t_hi, wr_hi), (x2t_hi, wr_lo), (x2t_lo, wr_hi))):
                                last = pe.matmul(misc_ps[:, RC * i:RC * i + RC], xs[:, b % 2, k, i * P:(i + 1) * P], ws[:, k, :],
                                                 start=(k == 0 and m == 0), stop=(k == KC - 1 and m == 2))
                    last.then_inc(s["logits_ready"], 1)
                b = after_batch(n, 7)
                if b is not None:
                    pe.wait_ge(s["sel_ready"], b + 1)
                    if b == 0:
                        pe.wait_ge(s["routing_ready"], 1)
                    for i in range(TB):
                        pe.matmul(misc_ps[:, NE * i:NE * i + NE], ones_b[:, :], sofar_b[:, i, :], start=True, stop=False)
                        last = pe.matmul(misc_ps[:, NE * i:NE * i + NE], before_b[:, :], sel_b[:, i, :], start=False, stop=True)
                    last.then_inc(s["excl_ready"], 1)
                b = after_batch(n, 8)
                if b is not None:
                    pe.wait_ge(s["pick_ready"], b + 1)
                    for j in range(NJ):
                        for i in range(TB):
                            pk = pick[:, TB * b + i, P * j:P * (j + 1)]
                            last = pe.matmul(misc_ps[:, 2 * j:2 * j + 2], pk, row_no[:, TB * b + i, :], start=(i == 0), stop=(i == TB - 1))
                    last.then_inc(s["idx_ready"], 1)
                bf_ = ffn_at(n, 0)
                if bf_:
                    b, f = bf_
                    m = NF * b + f
                    f0, w = FCH[f]
                    if m == 0:
                        pe.wait_ge(s["wshared_ready"], 4)
                    if f == 0:
                        pe.wait_ge(s["x2lo_ready"], b + 1)
                        pe.wait_ge(s["state_ready"], min(KC * (b + 2), KC * B))
                    if m >= 1:
                        pe.wait_ge(s["h_ready"], m)
                    for gu in range(2):
                        for k in range(KC):
                            for q, (ws, xs) in enumerate(((wu_hi, x2t_hi), (wu_hi, x2t_lo), (wu_lo, x2t_hi))):
                                last = pe.matmul(up_ps[0:w, gu * S:(gu + 1) * S], ws[:, k, gu, f0:f0 + w], xs[:, b % 2, k, :],
                                                 start=(k == 0 and q == 0), stop=(k == KC - 1 and q == 2))
                    last.then_inc(s["up_ready"], 1)
                bf_ = ffn_at(n, 2)
                if bf_:
                    b, f = bf_
                    m = NF * b + f
                    w = FCH[f][1]
                    pe.wait_ge(s["hlo_ready"], m + 1)
                    if f == 0 and b > 0:
                        pe.wait_ge(s["base_ready"], b)
                    for i in range(TB):
                        for q, (hs, ws) in enumerate(((h_hi, wd_hi), (h_hi, wd_lo), (h_lo, wd_hi))):
                            last = pe.matmul(down_ps[:, i * H:(i + 1) * H], hs[0:w, m % 3, i * P:(i + 1) * P], ws[0:w, f, :],
                                             start=(f == 0 and i == 0 and q == 0), stop=(f == NF - 1 and q == 2), skip_group_check=True)
                    last.then_inc(s["downf_done"], 1)

            def rows_T(j):
                pe.wait_ge(xe_in[j % NX], 16 * (j // NX + 1))
                if j == 0:
                    pe.wait_ge(s["idx_added"], B)
                else:
                    pe.wait_ge(s["eht_evac"], j)
                xv = xe[:, j % NX, 0:H].rearrange("p (m k) -> p k m", k=KC)
                for k in range(KC):
                    last = pe.transpose(misc_ps[:, k * P:(k + 1) * P], xv[:, k, :], ident[:, :])
                last.then_inc(s["xet_ready"], 1)

            def back_T(j):
                if j == 0:
                    pe.wait_ge(s["h_ready"], NF * B)
                else:
                    pe.wait_ge(s["back_evac"], j)
                for t in range(NT):
                    pk = pick[:, t, P * j:P * (j + 1)]
                    last = pe.transpose(back_ps[:, :].bitcast(BF16)[:, t * P:(t + 1) * P], pk, ident_b[:, :])
                last.then_inc(s["back_ready"], 1)

            def expert_up(j):
                pe.wait_ge(s["xet_evac"], j + 1)
                pe.wait_ge(slot_in[j % NS], 48 * (j // NS + 1))
                if j == 0:
                    pe.wait_ge(s["norm1"], NT)
                else:
                    pe.wait_ge(s["eh_ready"], j)
                for k in range(KC):
                    for e in range(EG):
                        last = pe.matmul(eup_ps[32 * e:32 * e + 32, 0:2 * F], xeT[:, j % 2, k, 32 * e:32 * e + 32], we_up[j % NS][:, e, :, k, :],
                                         start=(k == 0), stop=(k == KC - 1), skip_group_check=True)
                last.then_inc(s["eup_ready"], 1)

            def hidden_T(j):
                pe.wait_ge(s["eh_ready"], j + 1)
                ev = eh[:, :].rearrange("p (m k) -> p k m", k=2)
                for k in range(2):
                    last = pe.transpose(misc_ps[0:FK, k * P:(k + 1) * P], ev[:, k, :], ident[:, :])
                last.then_inc(s["eht_ready"], 1)

            def expert_down(j):
                pe.wait_ge(s["eht_evac"], j + 1)
                if j == 0:
                    pe.wait_ge(s["base_ready"], B)
                else:
                    pe.wait_ge(s["ylo_ready"], j)
                for k in range(2):
                    for e in range(EG):
                        last = pe.matmul(edn_ps[32 * e:32 * e + 32, 0:H], ehT[:, k, 32 * e:32 * e + 32], we_dn[j % NS][0:FK, e, k, :],
                                         start=(k == 0), stop=(k == 1), skip_group_check=True)
                last.then_inc(s["edn_ready"], 1)

            def combine(j):
                pe.wait_ge(s["back_evac"], j + 1)
                pe.wait_ge(s["ylo_ready"], j + 1)
                if j == 0:
                    pe.wait_ge(s["pv_evac"], NT)
                for t in range(NT):
                    for q, ys in enumerate((y_hi, y_lo)):
                        last = pe.matmul(acc_ps[t // 2][:, (t % 2) * H:(t % 2 + 1) * H], back[:, j % 2, t * P:(t + 1) * P], ys[:, j % 2, :],
                                         start=(j == 0 and q == 0 and t % 2 == 0), stop=(j == NJ - 1 and q == 1), skip_group_check=True)
                    if j == NJ - 1 and t % 2 == 1:
                        last.then_inc(s["acc_ready"], 1)
                if j < NJ - 1:
                    last.then_inc(s["comb_done"], 1)

            for j in range(-1, NJ):
                if j + 1 < NJ:
                    rows_T(j + 1)
                    back_T(j + 1)
                    expert_up(j + 1)
                if j >= 0:
                    combine(j)
                if j + 1 < NJ:
                    hidden_T(j + 1)
                    expert_down(j + 1)

        @block.vector
        def _(dve):
            count = [0]

            def link(ins):
                count[0] += 1
                ins.then_inc(s["dve_chain"], 1)
                dve.wait_ge(s["dve_chain"], count[0])

            def head_values(b):
                dve.wait_ge(ctx_in[b], 16)
                cv = ctx_sb[:, TB * b:TB * b + TB, :].rearrange("p i (h d) -> p i h d", d=DH)
                if b > 0:
                    dve.wait_ge(s["vaug_ready"], b)
                link(dve.tensor_reduce(vmean[:, :, :], cv, AX.X, ALU.add))
                link(dve.tensor_scalar(vmean[:, :, :], vmean[:, :, :], 1.0 / DH, None, ALU.mult))
                if b >= 2:
                    dve.wait_ge(s["pv_done"], UB * (b - 1))
                for i in range(TB):
                    ins = dve.tensor_tensor(vaug[:, b % 2, i, :, 0:DH], cv[:, i, :, :], vmean[:, i, :].unsqueeze(2).broadcast_to([P, NH, DH]), ALU.subtract)
                ins.then_inc(s["vaug_ready"], 1)

            dve.memset(gw[:, :, :, :], 0.0).then_inc(s["pads_zero"], 1)
            dve.memset(bias[:, :], 0.0).then_inc(s["pads_zero"], 1)
            dve.memset(wr_raw[:, :, :], 0.0).then_inc(s["pads_zero"], 1)
            dve.memset(arg_l[:, :, :], -1.0).then_inc(s["minus_ready"], 1)
            dve.memset(vaug[:, :, :, :, DH:DH + 1], 1.0)
            dve.memset(vaug[:, :, :, :, DH + 1:HP], 0.0).then_inc(s["vpads_ready"], 1)
            link(dve.memset(sofar[:, :], 0.0))
            link(dve.memset(idxf[:, :, :], 0.0))
            link(dve.memset(aa[:, :], 1.0))
            for step in range(B + 1):
                if step < B:
                    b = step
                    dve.wait_ge(x_in[b], 16)
                    for t in range(TB * b, TB * b + TB):
                        link(dve.bn_stats(stats[:, t, :], x_sb[:, t, :]))
                        ins = dve.bn_aggr(mv[:, t, :], stats[:, t, :])
                    ins.then_inc(s["ln1_stats"], 1)
                if step > 0:
                    b = step - 1
                    dve.wait_ge(s["ln1_rstd"], b + 1)
                    for t in range(TB * b, TB * b + TB):
                        ins = dve.tensor_scalar(qn[:, t, :], x_sb[:, t, :], mv[:, t, 0:1], rstd[:, t:t + 1], ALU.subtract, ALU.mult)
                    ins.then_inc(s["qn_ready"], 1)
            dve.wait_ge(s["ident_ready"], 1)
            dve.tensor_copy(ident_b[:, :], ident[:, :]).then_inc(s["identb_ready"], 1)
            dve.wait_ge(s["heads_made"], 2)
            dve.tensor_copy(headsel[:, :, :, :].rearrange("p b c (h d) -> p (b c h) d", d=DH),
                            batch_heads[:, :, :, :].rearrange("p b c h -> p (b c h)").unsqueeze(2).broadcast_to([P, B * NH, DH]))
            link(dve.tensor_scalar(blockmask[:, :, :], row_head[:, :, :].rearrange("p a h -> p (a h)").unsqueeze(2).broadcast_to([P, HC, HP]),
                                   float(DH) ** -0.5, None, ALU.mult))
            dve.memset(th[:, 0, 0:1], 0.0).then_inc(s["masks_ready"], 1)
            head_values(0)
            head_values(1)
            dve.wait_ge(s["gates_ready"], 1)
            dve.wait_ge(bias_in, 32 * B)
            dve.tensor_scalar(ig[:, :], misc_ps[:, 0:S], bias[:, 0:1], None, ALU.add)
            link(dve.tensor_scalar(g2[:, :], misc_ps[:, S:2 * S], bias[:, 1:2], None, ALU.add))
            dve.scalar_tensor_tensor(g1[:, :], g2[:, :], -1.0, g2[:, :], ALU.mult, ALU.max).then_inc(s["gates_ln_in"], 1)
            link(dve.tensor_scalar(cum[:, :], g2[:, :], 0.0, None, ALU.min))
            dve.wait_ge(s["gates_l"], 1)
            link(dve.tensor_tensor(g2[:, :], cum[:, :], nm[:, :], ALU.subtract))
            link(dve.tensor_tensor_scan(cum[:, :], aa[:, :], g2[:, :], 0.0, ALU.mult, ALU.add))
            link(dve.tensor_tensor(aa[:, :], ig[:, :], cum[:, :], ALU.subtract))
            link(dve.tensor_tensor_scan(mm_[:, :], aa[:, :], aa[:, :], -3.0e38, ALU.max, ALU.max))
            link(dve.tensor_scalar(negA0[:, :], mm_[:, P - 1:P], -1.0, None, ALU.mult))
            dve.tensor_tensor(nm[:, :], cum[:, :], mm_[:, :], ALU.add).then_inc(s["a_ready"], 1)
            for src, parts in ((aa, a_part), (mm_, m_part)):
                link(dve.tensor_copy(parts[:, 0, :], src[:, :]))
                link(dve.tensor_tensor(g1[:, :], src[:, :], parts[:, 0, :], ALU.subtract))
                link(dve.tensor_copy(parts[:, 1, :], g1[:, :]))
                link(dve.tensor_tensor(g2[:, :], g1[:, :], parts[:, 1, :], ALU.subtract))
                dve.tensor_copy(parts[:, 2, :], g2[:, :]).then_inc(s["parts_ready"], 1)

            for n in range(LAST + 1):
                if n < NU:
                    dve.wait_ge(s["d_ready"], n + 1)
                    dve.wait_ge(s["qk_ready"], n + 1)
                    if n >= 2:
                        dve.wait_ge(s["pv_done"], n - 1)
                    dve.scalar_tensor_tensor(cc[:, n % 2, :, :].rearrange("p h t -> p (h t)"), qk_ps[n % 2][:, :], float(DH) ** -0.5,
                                             dd[:, n % 2, :, :].rearrange("p h t -> p (h t)"), ALU.mult, ALU.mult).then_inc(s["c_ready"], 1)
                b, u = divmod(n, UB)
                if b < B and u in (3, 4):
                    c = u - 3
                    dve.wait_ge(s["st_ready"], KC * b + c + 1)
                    if b > 0:
                        dve.wait_ge(s["pv_done"], UB * (b - 1) + NG + (NG // KC) * (c + 1))
                    dve.tensor_tensor(state[:, c, :, :].rearrange("p h e -> p (h e)"), up_ps[:, 0:HC * HP], blockmask[:, :, :].rearrange("p h e -> p (h e)"), ALU.mult)
                    dve.tensor_tensor(qr[:, c, :], up_ps[:, HC * HP:HC * HP + P], qT[:, c, tok(b, 1)], ALU.mult).then_inc(s["state_ready"], 1)
                if b >= 1 and b + 1 < B and u == 2:
                    head_values(b + 1)
                k = (n - 5) // 4
                if n >= 5 and (n - 5) % 4 == 0 and k < NT:
                    b, i = divmod(k, TB)
                    dve.wait_ge(s["ht_ready"], k + 1)
                    if k == 0:
                        dve.wait_ge(s["wtnm_ready"], 2)
                    d, v, q = den[:, k % 2, :], inv[:, k % 2, :], hv[:, k % 2, :, :]
                    bound = wtnm[:, 1 + i, 32 * b:32 * b + NH]
                    link(dve.scalar_tensor_tensor(d, ht3[:, :, DH], 1e-6, bound, ALU.subtract, ALU.max, reverse0=True))
                    link(dve.scalar_tensor_tensor(d, ht3[:, :, DH], 1e-6, d, ALU.add, ALU.max))
                    link(dve.reciprocal(v, d))
                    link(dve.tensor_tensor(q, ht3[:, :, 0:DH], v.unsqueeze(2).broadcast_to([P, NH, DH]), ALU.mult))
                    link(dve.tensor_tensor(sq[:, :, :], q, q, ALU.mult))
                    link(dve.tensor_reduce(ssq[:, k % 2, :], sq[:, :, :], AX.X, ALU.add))
                    dve.tensor_scalar(ssq[:, k % 2, :], ssq[:, k % 2, :], 1.0 / DH, 1e-6, ALU.mult, ALU.add).then_inc(s["norm1"], 1)
                    if k == 0:
                        dve.wait_ge(ln_in, 16)
                    link(dve.tensor_tensor(q, q, ln_bc[:, :].rearrange("p (h d) -> p h d", d=DH), ALU.mult))
                k = (n - 6) // 4
                if n >= 6 and (n - 6) % 4 == 0 and k < NT:
                    dve.wait_ge(s["norm_rs"], k + 1)
                    link(dve.tensor_tensor(yy[:, k % 2, :].rearrange("p (h d) -> p h d", d=DH), hv[:, k % 2, :, :],
                                           rs[:, k % 2, :].unsqueeze(2).broadcast_to([P, NH, DH]), ALU.mult))
                    dve.tensor_tensor(x_sb[:, k, :], x_sb[:, k, :], yy[:, k % 2, :], ALU.add).then_inc(s["x_new"], 1)
                    dve.wait_ge(s["x_new"], k + 1)
                    link(dve.bn_stats(stats[:, k, :], x_sb[:, k, :]))
                    dve.bn_aggr(mv[:, k, :], stats[:, k, :]).then_inc(s["ln2_stats"], 1)
                k = (n - 7) // 4
                if n >= 7 and (n - 7) % 4 == 0 and k < NT:
                    b, i = divmod(k, TB)
                    dve.wait_ge(s["ln2_rstd"], k + 1)
                    if b >= 2:
                        dve.wait_ge(rows_out[b - 2], 16)
                    dve.tensor_scalar(x2w[:, b % 2, i, 0:H], x_sb[:, k, :], mv[:, k, 0:1], rstd[:, k:k + 1], ALU.subtract, ALU.mult).then_inc(s["x2_ready"], 1)
                b = after_batch(n, 4)
                if b is not None:
                    dve.wait_ge(s["x2hi_ready"], b + 1)
                    dve.tensor_tensor(x2t_lo[:, b % 2, :, :].rearrange("p c t -> p (c t)"), misc_ps[:, :],
                                      x2t_hi[:, b % 2, :, :].rearrange("p c t -> p (c t)").bitcast(F32), ALU.subtract).then_inc(s["x2lo_ready"], 1)
                b = after_batch(n, 5)
                if b is not None:
                    dve.wait_ge(s["logits_ready"], b + 1)
                    if b == 0:
                        dve.wait_ge(s["routing_ready"], 1)
                    link(dve.tensor_copy(lg[:, :, :].rearrange("p i c -> p (i c)"), misc_ps[:, 0:TB * RC]))
                    for i in range(TB):
                        link(dve.max(m8[:, i, :], lg[:, i, 0:NE]))
                        link(dve.max_index(i8[:, i, :], m8[:, i, :], lg[:, i, 0:NE]))
                    dve.tensor_scalar(nmax[:, :], m8[:, :, 0], -1.0, None, ALU.mult).then_inc(s["nmax_ready"], 1)
                    link(dve.tensor_copy(i8f[:, :, :], i8[:, :, :]))
                    for i in range(TB):
                        link(dve.tensor_tensor(eq4[:, :, :], expert_no[:, :].unsqueeze(2).broadcast_to([P, NE, TOPK]),
                                               i8f[:, i, 0:TOPK].unsqueeze(1).broadcast_to([P, NE, TOPK]), ALU.is_equal))
                        link(dve.tensor_reduce(sel[:, i, :], eq4[:, :, :], AX.X, ALU.add))
                        dve.tensor_copy(sel_b[:, i, :], sel[:, i, :])
                        link(dve.tensor_copy(sofar_b[:, i, :], sofar[:, :]))
                        ins = dve.tensor_tensor(sofar[:, :], sofar[:, :], sel[:, i, :], ALU.add)
                        if i < TB - 1:
                            link(ins)
                    ins.then_inc(s["sel_ready"], 1)
                    dve.wait_ge(s["sel_ready"], b + 1)
                b = after_batch(n, 6)
                if b is not None:
                    dve.wait_ge(s["ex_ready"], TB * (b + 1))
                    for i in range(TB):
                        link(dve.scalar_tensor_tensor(ex[:, i, :], ex[:, i, :], 1.0, sel[:, i, :], ALU.mult, ALU.mult, accum_out=ssum[:, i:i + 1]))
                    link(dve.reciprocal(rsum[:, :], ssum[:, :]))
                    for i in range(TB):
                        ins = dve.tensor_scalar(x2w[:, b % 2, i, H:XW], ex[:, i, :], rsum[:, i:i + 1], None, ALU.mult)
                    ins.then_inc(s["rw_ready"], 1)
                    dve.wait_ge(s["gate_th"], b + 1)
                    link(dve.tensor_scalar(gate[:, TB * b:TB * b + TB], gate[:, TB * b:TB * b + TB], 0.5, 0.5, ALU.mult, ALU.add))
                b = after_batch(n, 7)
                if b is not None:
                    dve.wait_ge(s["excl_ready"], b + 1)
                    link(dve.tensor_scalar(vt[:, :, :].rearrange("p i e -> p (i e)"), misc_ps[:, 0:TB * NE], 64.0, 128.0, ALU.min, ALU.add))
                    link(dve.scalar_tensor_tensor(vb[:, :, :].rearrange("p i e -> p (i e)"), sel[:, :, :].rearrange("p i e -> p (i e)"), -128.0,
                                                  vt[:, :, :].rearrange("p i e -> p (i e)"), ALU.mult, ALU.add))
                    for i in range(TB):
                        ins = dve.tensor_tensor(pick[:, TB * b + i, :].rearrange("p (e c) -> p e c", c=CAP), vb[:, i, :].unsqueeze(2).broadcast_to([P, NE, CAP]),
                                                slot_no[:, :].unsqueeze(1).broadcast_to([P, NE, CAP]), ALU.is_equal)
                    ins.then_inc(s["pick_ready"], 1)
                b = after_batch(n, 9)
                if b is not None:
                    dve.wait_ge(s["idx_ready"], b + 1)
                    dve.tensor_tensor(idxf[:, :, :].rearrange("p j a -> p (j a)"), misc_ps[:, 0:2 * NJ], idxf[:, :, :].rearrange("p j a -> p (j a)"), ALU.add).then_inc(s["idx_added"], 1)
                    if b == B - 1:
                        dve.wait_ge(s["idx_added"], B)
                        dve.tensor_tensor(idx[:, :], idxf[:, :, 0], idxf[:, :, 1], ALU.add).then_inc(s["idx_int"], 1)
                bf_ = ffn_at(n, 0)
                if bf_:
                    b, f = bf_
                    m = NF * b + f
                    w = FCH[f][1]
                    dve.wait_ge(s["th_ready"], m + 1)
                    link(dve.scalar_tensor_tensor(s1[0:w, m % 2, :], th[0:w, m % 2, :], 1.0, up_ps[0:w, 0:S], ALU.add, ALU.mult))
                    if m >= 2:
                        dve.wait_ge(s["hlo_ready"], m - 1)
                    dve.scalar_tensor_tensor(hf[0:w, m % 2, :], s1[0:w, m % 2, :], 0.5, up_ps[0:w, S:2 * S], ALU.mult, ALU.mult).then_inc(s["h_ready"], 1)
                bf_ = ffn_at(n, 2)
                if bf_ and bf_[1] == NF - 1:
                    b = bf_[0]
                    dve.wait_ge(s["downf_done"], NF * (b + 1))
                    for i in range(TB):
                        t = TB * b + i
                        ins = dve.scalar_tensor_tensor(x_sb[:, t, :], down_ps[:, i * H:(i + 1) * H], gate[:, t:t + 1], x_sb[:, t, :], ALU.mult, ALU.add)
                    ins.then_inc(s["base_ready"], 1)

            for j in range(NJ):
                dve.wait_ge(xe_in[j % NX], 16 * (j // NX + 1))
                link(dve.tensor_tensor(w4[:, j, :], xe[:, j % NX, H + EG * j:H + EG * j + EG], own_expert[:, j, :], ALU.mult))
                dve.tensor_reduce(wslot[:, j:j + 1], w4[:, j, :], AX.X, ALU.add).then_inc(s["wslot_ready"], 1)
                dve.wait_ge(s["eth_ready"], j + 1)
                link(dve.scalar_tensor_tensor(es1[:, :], eth[:, :], 1.0, eup_ps[:, 0:F], ALU.add, ALU.mult))
                if j > 0:
                    dve.wait_ge(s["eht_ready"], j)
                dve.scalar_tensor_tensor(eh[:, :], es1[:, :], 0.5, eup_ps[:, F:2 * F], ALU.mult, ALU.mult).then_inc(s["eh_ready"], 1)
                dve.wait_ge(s["eht_ready"], j + 1)
                if j > 0:
                    dve.wait_ge(s["edn_ready"], j)
                dve.tensor_copy(ehT[:, :, :].rearrange("p k t -> p (k t)"), misc_ps[0:FK, 0:2 * P]).then_inc(s["eht_evac"], 1)
                dve.wait_ge(s["yhi_ready"], j + 1)
                dve.scalar_tensor_tensor(y_lo[:, j % 2, :], edn_ps[:, 0:H], wslot[:, j:j + 1], y_hi[:, j % 2, :].bitcast(F32), ALU.mult, ALU.subtract).then_inc(s["ylo_ready"], 1)
            for q in range(4):
                dve.wait_ge(s["acc_ready"], q + 1)
                xv = x_sb[:, TB * q:TB * q + TB, :].rearrange("p i h -> p (i h)")
                dve.tensor_tensor(xv, acc_ps[q][:, :], xv, ALU.add).then_inc(s["final_ready"], 1)


_INS = ['x', 'ctx_2048', 'L0_xattn_Wi', 'L0_xattn_bi', 'L0_xattn_Wf', 'L0_xattn_bf', 'L0_xattn_ln_scale', 'L0_ffn_Wr', 'L0_ffn_Wg',
        'L0_ffn_Wu', 'L0_ffn_Wd', 'L0_ffn_Wsg', 'L0_ffn_Wsu', 'L0_ffn_Wsd', 'L0_ffn_Wse']
_OUTS = [((4, 256, 256), 'float32')]


def kernel(**inputs):
    import numpy as _np
    import concourse.bacc as _bacc
    from concourse import mybir as _mybir
    from concourse.bass_utils import run_bass_kernel_spmd as _run

    nc = _bacc.Bacc("TRN2", target_bir_lowering=False, num_devices=1)
    arrays, args = {}, []
    for name in _INS:
        a = _np.ascontiguousarray(inputs[name])
        arrays[f"in_{name}_dram"] = a
        args.append(nc.dram_tensor(f"in_{name}_dram", a.shape, _mybir.dt.from_np(a.dtype), kind="ExternalInput").ap())
    for i, (shape, dtype) in enumerate(_OUTS):
        dt = _mybir.dt.from_np(_np.dtype(dtype))
        args.append(nc.dram_tensor(f"out_{i}_dram", shape, dt, kind="ExternalOutput").ap())
    xattn_moe_kernel(nc, *args)
    r = _run(nc, [arrays], core_ids=[0])
    got = tuple(r.results[0][f"out_{i}_dram"] for i in range(len(_OUTS)))
    return got[0]
```

```python
import concourse.bass as bass
from concourse import mybir
from contextlib import ExitStack

ALU = mybir.AluOpType
ACT = mybir.ActivationFunctionType
AX = mybir.AxisListType
F32 = mybir.dt.float32
F32R = mybir.dt.float32r
BF16 = mybir.dt.bfloat16
U32 = mybir.dt.uint32
I32 = mybir.dt.int32

P = 128
NEG = -1.0e30


def xattn_moe_kernel(nc: bass.Bass, x, ctx, Wi, bi, Wf, bf, ln_scale, Wr, Wg, Wu, Wd, Wsg, Wsu, Wsd, Wse, out):
    B, S, H = x.shape
    NH = Wi.shape[1]
    DH = H // NH
    NE, _, F = Wg.shape
    FS = Wsg.shape[1]
    TOPK = 4
    CAP = 32
    TB = S // P
    NT = B * TB
    KC = H // P
    HC = NH // KC
    GH = 4
    NG = NH // GH
    UB = TB * NG
    NU = B * UB
    HP = 32
    FCH = [(c, min(P, FS - c)) for c in range(0, FS, P)]
    NF = len(FCH)
    EG = P // CAP
    NJ = NE // EG
    FK = F // 2
    RC = NE + 2
    XW = H + NE
    LAST = NU + 13
    assert (B, S, H, NH, NE, F) == (4, 256, 256, 16, 32, 176) and TB == KC == 2 and DH == 16

    rows = nc.dram_tensor("routed_rows", (NT * P, XW), F32, kind="Internal").ap()

    with ExitStack() as es:
        at = [16512]

        def place(name, shape, dt, where=None):
            size = 2 if dt == BF16 else 4
            for n in shape[1:]:
                size *= n
            size = -(-size // 32) * 32
            if where is None:
                where = at[0]
                at[0] += size
            assert where + size <= 229344, (name, where + size)
            return nc.alloc_sbuf_tensor_at(name, shape, dt, offset=where)

        def sem(name):
            return es.enter_context(nc.semaphore(name))

        x_sb = place("x_sb", [P, NT, H], F32)
        pick_at = at[0]
        pick = place("pick", [P, NT, CAP * NE], BF16)
        qn = place("qn", [P, NT, H], F32, pick_at)
        wu_hi_at = at[0]
        tail = FCH[-1][1]
        wu_hi = place("wu_hi", [P, KC, 2, FS - tail], F32R)
        wut_hi = place("wut_hi", [P, KC, 2 * tail], F32R)
        wu_lo = place("wu_lo", [P, KC, 2, FS - tail], F32R)
        wut_lo = place("wut_lo", [P, KC, 2 * tail], F32R)
        wd_hi = place("wd_hi", [P, NF, H], F32R)
        wd_lo = place("wd_lo", [P, NF, H], F32R)
        wr_raw = place("wr_raw", [P, KC, RC], F32)
        wr_hi = place("wr_hi", [P, KC, RC], F32R)
        wr_lo = place("wr_lo", [P, KC, RC], F32R)
        x2t_hi = place("x2t_hi", [P, 2, KC, S], F32R)
        x2t_lo = place("x2t_lo", [P, 2, KC, S], F32R)
        x2w = place("x2w", [P, 2, TB, XW], F32)
        th = place("th", [P, 2, S], F32)
        s1 = place("s1", [P, 2, S], F32)
        hf = place("hf", [P, 2, S], F32)
        h_hi = place("h_hi", [P, 3, S], F32R)
        h_lo = place("h_lo", [P, 3, S], F32R)
        ident = place("ident", [P, P], F32)
        head_rows = place("head_rows", [P, KC, HC], BF16)
        batch_heads = place("batch_heads", [P, B, KC, HC], F32)
        row_head = place("row_head", [P, 2, GH], F32)
        ident_b = place("ident_b", [P, P], BF16)
        before_b = place("before_b", [P, P], BF16)
        ones_b = place("ones_b", [P, P], BF16)
        slot_no = place("slot_no", [P, CAP], BF16)
        expert_no = place("expert_no", [P, NE], F32)
        row_no = place("row_no", [P, NT, 2], BF16)
        own_expert = place("own_expert", [P, NJ, EG], F32)
        mhalf = place("mhalf", [P, NH], F32)
        ln_bc = place("ln_bc", [P, H], F32)
        stats = place("stats", [P, NT, 6], F32)
        mv = place("mv", [P, NT, 2], F32)
        rstd = place("rstd", [P, NT], F32)
        lg = place("lg", [P, TB, RC], F32)
        m8 = place("m8", [P, TB, 8], F32)
        i8 = place("i8", [P, TB, 8], U32)
        i8f = place("i8f", [P, TB, 8], F32)
        eq4 = place("eq4", [P, TB, NE, TOPK], F32)
        sel = place("sel", [P, TB, NE], F32)
        sel_b = place("sel_b", [P, TB, NE], BF16)
        nmax = place("nmax", [P, TB], F32)
        ex = place("ex", [P, TB, NE], F32)
        ssum = place("ssum", [P, TB], F32)
        rsum = place("rsum", [P, TB], F32)
        gate = place("gate", [P, NT], F32)
        sofar = place("sofar", [P, NT + 1, NE], BF16)
        vt = place("vt", [P, TB, NE], F32)
        vb = place("vb", [P, TB, NE], BF16)
        idxf = place("idxf", [P, NJ, 2], F32)
        idx = place("idx", [P, NJ], I32)
        w4 = place("w4", [P, NJ, EG], F32)
        wslot = place("wslot", [P, NJ], F32)
        slot0_at = at[0]
        stage_u = place("stage_u", [P, KC, 2, FS], F32)
        stage_d_at = at[0]
        at[0] = slot0_at + 4 * (EG * 2 * KC * F + EG * 2 * H)
        stage_d = place("stage_d", [P, NF, H], F32, stage_d_at)

        att_at = at[0]
        ctx_sb = place("ctx_sb", [P, NT, H], F32)
        qT = place("qT", [P, KC, B * S], F32)
        ctxT = place("ctxT", [P, KC, B * S], F32)
        qbd = place("qbd", [P, KC, HC, S], F32)
        vaug = place("vaug", [P, 2, TB, NH, HP], F32)
        arg_r = place("arg_r", [51, 2, HC, S], BF16)
        arg_l = place("arg_l", [51, B, S], BF16)
        dd = place("dd", [P, 2, GH, P], F32)
        cc = place("cc", [P, 2, GH, P], F32)
        hT = place("hT", [P, 2, NG, P], F32)
        state = place("state", [P, 2, HC, HP], F32)
        qr = place("qr", [P, 2, P], F32)
        wv = place("wv", [P, 2, HC, HP], F32)
        headsel = place("headsel", [P, B, KC, P], F32)
        wtnm = place("wtnm", [P, 3, P], F32)
        gw = place("gw", [P, 3 * KC, 2, 32], F32)
        bias = place("bias", [P, 2], F32)
        causal = place("causal", [P, P], BF16)
        blockmask = place("blockmask", [P, HC, HP], F32)
        vmean = place("vmean", [P, TB, NH], F32)
        ig = place("ig", [P, S], F32)
        g1 = place("g1", [P, S], F32)
        g2 = place("g2", [P, S], F32)
        cum = place("cum", [P, S], F32)
        aa = place("aa", [P, S], F32)
        mm_ = place("mm_", [P, S], F32)
        nm = place("nm", [P, S], F32)
        wfac = place("wfac", [P, P], F32)
        rfac = place("rfac", [P, P], F32)
        a_part = place("a_part", [P, 3, S], BF16)
        m_part = place("m_part", [P, 3, S], BF16)
        negA0 = place("negA0", [P, 1], F32)
        den = place("den", [P, 2, NH], F32)
        inv = place("inv", [P, 2, NH], F32)
        hv = place("hv", [P, 2, NH, DH], F32)
        ssq = place("ssq", [P, 2, NH], F32)
        rs = place("rs", [P, 2, NH], F32)
        yy = place("yy", [P, NH, DH], F32)
        att_end = at[0]

        up_bytes, down_bytes = 4 * EG * 2 * KC * F, 4 * EG * 2 * H
        slots_at = [slot0_at] + [att_at + n * (up_bytes + down_bytes) for n in range(3)] + [wu_hi_at]
        NS = len(slots_at)
        we_up = [place(f"we_up{n}", [P, EG, 2, KC, F], F32, a) for n, a in enumerate(slots_at)]
        we_dn = [place(f"we_dn{n}", [P, EG, 2, H], F32, a + up_bytes) for n, a in enumerate(slots_at)]
        at[0] = att_at + 3 * (up_bytes + down_bytes)
        NX = NJ
        back = place("back", [P, 2, NT * P], F32R)
        xe = place("xe", [P, NX, XW], F32)
        xeT = place("xeT", [P, 2, KC, P], F32)
        eth = place("eth", [P, F], F32)
        es1 = place("es1", [P, F], F32)
        eh = place("eh", [P, F], F32)
        ehT = place("ehT", [FK, 2, P], F32)
        y_hi = place("y_hi", [P, 2, H], F32R)
        y_lo = place("y_lo", [P, 2, H], F32R)
        assert at[0] <= 229344, at[0]

        bank = [es.enter_context(nc.psum_tensor(f"bank{n}", [P, 512], F32)) for n in range(8)]
        qk_ps, arg_ps, pv_ps, ht_ps, up_ps, down_ps, misc_ps = bank[0:2], bank[2], bank[3], bank[4], bank[5], bank[6], bank[7]
        acc_ps, eup_ps, back_ps, edn_ps = bank[0:4], bank[4], bank[5], bank[6]
        ht3 = ht_ps[:, :].rearrange("p (h e) -> p h e", e=HP)

        x_in = [sem(f"x_in{b}") for b in range(B)]
        ctx_in = [sem(f"ctx_in{b}") for b in range(B)]
        gw_in, bias_in, ln_in, wr_in, stage_in = map(sem, ("gw_in", "bias_in", "ln_in", "wr_in", "stage_in"))
        argl_in = [sem(f"argl_in{b}") for b in range(B)]
        argr_in = [sem(f"argr_in{c}") for c in range(KC)]
        slot_in = [sem(f"slot_in{n}") for n in range(NS)]
        rows_out = [sem(f"rows_out{b}") for b in range(B)]
        out_done = sem("out_done")
        xe_in = [sem(f"xe_in{n}") for n in range(NX)]
        names = ("dve_chain act_chain pool_chain pads_zero minus_ready vpads_ready ident_ready identb_ready rows_made heads_made selector_ready "
                 "masks_made routing_ready masks_ready ln1_stats ln1_rstd qn_ready "
                 "tposed t_evac gates_ready gates_ln_in gates_e gates_l a_ready fac_ready parts_ready fact_ready wtnm_ready gw_summed "
                 "vaug_ready wv_ready qbd_ready arg_ready d_ready qk_ready c_ready pv_done pv_evac ht_ready norm1 norm_rs "
                 "x_new ln2_stats ln2_rstd x2_ready st_ready state_ready x2t_ready x2hi_ready x2lo_ready logits_ready "
                 "nmax_ready ex_ready sel_ready rw_ready excl_ready pick_ready idx_ready idx_added up_ready th_ready "
                 "h_ready hhi_ready hlo_ready downf_done base_ready wshared_ready wr_ready idx_int "
                 "xet_ready xet_evac eup_ready eth_ready eh_ready eht_ready eht_evac edn_ready yhi_ready ylo_ready "
                 "back_ready back_evac comb_done acc_ready final_ready wslot_ready gate_th weight_hi hlo_last vmean_ready x2_last").split()
        s = {n: sem(n) for n in names}
        block = es.enter_context(nc.Block())

        weight_parts = [(wr_raw[:, :, :], wr_hi[:, :, :], wr_lo[:, :, :])]
        weight_parts += [(stage_u[:, k, :, 0:FS - tail], wu_hi[:, k, :, :], wu_lo[:, k, :, :]) for k in range(KC)]
        weight_parts += [(stage_u[:, :, :, FS - tail:FS].rearrange("p k g f -> p (k g) f"),
                          wut_hi[:, :, :].rearrange("p k (g f) -> p (k g) f", g=2), wut_lo[:, :, :].rearrange("p k (g f) -> p (k g) f", g=2))]
        weight_parts += [(stage_d[:, 0:NF - 1, :], wd_hi[:, 0:NF - 1, :], wd_lo[:, 0:NF - 1, :]),
                         (stage_d[0:tail, NF - 1, :], wd_hi[0:tail, NF - 1, :], wd_lo[0:tail, NF - 1, :])]

        def unit(n):
            b, u = divmod(n, UB)
            i, g = divmod(u, NG)
            return b, i, g, g // (NG // KC), g % (NG // KC)

        def tok(b, i):
            return slice(b * S + i * P, b * S + (i + 1) * P)

        def tile_at(n, lag):
            for k in range(NT):
                if n == 4 * k + lag + (1 if k < TB else 0):
                    return k
            return None

        up_steps, down_steps = {}, {}
        for b in range(B):
            for f in range(NF):
                step = (b + 1) * UB + 5 + f + (1 if b == 0 else 2 if b == B - 2 and f >= NF // 2 else 0)
                up_steps[step] = (b, f)
                down_steps[step + (2 if b == B - 2 and f >= NF // 2 else 3)] = (b, f)

        def ffn_at(n, lag):
            return up_steps.get(n - lag)

        def up_bank(n):
            if n > NU:
                return bank[0] if n % 2 else up_ps
            return up_ps if n % 2 else ht_ps

        def wait_up_used(engine, used, n):
            steps = [k for k in up_steps if k < n and up_bank(k) is used]
            if steps:
                b, f = up_steps[max(steps)]
                engine.wait_ge(s["h_ready"], NF * b + f + 1)

        def after_batch(n, u, last_u=None):
            if last_u is not None and n - B * UB in (u, last_u):
                return B - 1 if n - B * UB == last_u else None
            for b in range(B):
                if n == (b + 1) * UB + u + (1 if b == 0 else 0):
                    return b
            return None

        index_steps, added_steps = {}, {}
        for b in range(B):
            step = (b + 1) * UB + 9 + (1 if b == 0 else 2 if b == B - 2 else 0)
            index_steps[step] = b
            added_steps[step + (1 if b < B - 2 else 0)] = b

        def wait_low(engine, m):
            last = m >= NF * (B - 1)
            engine.wait_ge(s["hlo_last" if last else "hlo_ready"], m + 1 - (NF * (B - 1) if last else 0))

        def store_rows(engine, b):
            engine.dma_start(rows[b * S:(b + 1) * S, :].rearrange("(i p) w -> p i w", p=P), x2w[:, b % 2, :, :]).then_inc(rows_out[b], 16)

        @block.sync
        def _(sp):
            def load_x(b):
                sp.dma_start(x_sb[:, TB * b:TB * b + TB, :], x[b].rearrange("(i p) h -> p i h", p=P)).then_inc(x_in[b], 16)

            def load_ctx(b):
                sp.dma_start(ctx_sb[:, TB * b:TB * b + TB, :], ctx[b].rearrange("(i p) h -> p i h", p=P)).then_inc(ctx_in[b], 16)

            load_x(0)
            load_ctx(0)
            for b in range(1, B):
                load_x(b)
            sp.wait_ge(s["pads_zero"], 3)
            with nc.allow_non_contiguous_dma(reason="rows of 16 gates"):
                sp.dma_start(gw[:, :, 0, 0:NH], Wi.rearrange("(k p) g -> p k g", p=P)).then_inc(gw_in, 16)
                sp.dma_start(gw[:, :, 1, 0:NH], Wf.rearrange("(k p) g -> p k g", p=P)).then_inc(gw_in, 16)
                for b in range(1, B):
                    load_ctx(b)
                for b in range(B):
                    sp.dma_start(bias[32 * b:32 * b + NH, 0:1], bi.rearrange("(h a) -> h a", a=1)).then_inc(bias_in, 16)
                    sp.dma_start(bias[32 * b:32 * b + NH, 1:2], bf.rearrange("(h a) -> h a", a=1)).then_inc(bias_in, 16)
                sp.dma_start(wr_raw[:, :, 0:NE], Wr.rearrange("(k p) e -> p k e", p=P)).then_inc(wr_in, 16)
                sp.dma_start(wr_raw[:, :, NE:NE + 1], Wse.rearrange("(k p) e -> p k e", p=P)).then_inc(wr_in, 16)
            sp.dma_start(ln_bc[:, :], ln_scale.rearrange("(a h) -> a h", a=1).broadcast_to([P, H])).then_inc(ln_in, 16)
            sp.dma_start(stage_u[:, :, 0, :], Wsg.rearrange("(k p) f -> p k f", p=P)).then_inc(stage_in, 16)
            sp.dma_start(stage_u[:, :, 1, :], Wsu.rearrange("(k p) f -> p k f", p=P)).then_inc(stage_in, 16)
            sp.dma_start(stage_d[:, 0:NF - 1, :], Wsd[0:(NF - 1) * P, :].rearrange("(c p) h -> p c h", p=P)).then_inc(stage_in, 16)
            sp.dma_start(stage_d[0:FCH[-1][1], NF - 1, :], Wsd[(NF - 1) * P:FS, :]).then_inc(stage_in, 16)

            sp.wait_ge(s["minus_ready"], 1)
            sp.wait_ge(s["parts_ready"], 1)
            def load_arg_l(b):
                sp.dma_start(arg_l[0:3 * NH, b, :], a_part[32 * b:32 * b + NH, :, :]).then_inc(argl_in[b], 16)

            def load_arg_r(b, c):
                if b > 0:
                    sp.wait_ge(s["arg_ready"], UB * (b - 1) + NG + (NG // KC) * (c + 1))
                for part in range(3):
                    sp.dma_start(arg_r[48 + part:49 + part, c, :, :], m_part[32 * b + HC * c:32 * b + HC * c + HC, part, :]).then_inc(argr_in[c], 16)

            def load_slot(j):
                n = j % NS
                sp.dma_start(we_up[n][:, :, 0, :, :], Wg[EG * j:EG * j + EG].rearrange("e (p k) f -> p e k f", k=KC)).then_inc(slot_in[n], 16)
                sp.dma_start(we_up[n][:, :, 1, :, :], Wu[EG * j:EG * j + EG].rearrange("e (p k) f -> p e k f", k=KC)).then_inc(slot_in[n], 16)
                sp.dma_start(we_dn[n][0:FK, :, :, :], Wd[EG * j:EG * j + EG].rearrange("e (p k) h -> p e k h", k=2)).then_inc(slot_in[n], 16)

            load_arg_l(0)
            sp.wait_ge(s["parts_ready"], 2)
            for part in range(3):
                sp.dma_start(arg_r[48 + part:49 + part, :, :, :], m_part[0:NH, part, :]).then_inc(argr_in[0], 16)
            for b in range(1, B):
                load_arg_l(b)
            for c in range(KC):
                load_arg_r(1, c)
            sp.wait_ge(s["wshared_ready"], len(weight_parts) - 1)
            load_slot(0)
            for b in range(2, B):
                for c in range(KC):
                    load_arg_r(b, c)
            sp.wait_ge(s["pv_done"], NU)
            sp.wait_ge(s["ht_ready"], NT)
            sp.wait_ge(s["norm1"], NT)
            sp.wait_ge(s["x_new"], NT)
            load_slot(1)
            sp.wait_ge(s["rw_ready"], B)
            store_rows(sp, B - 1)
            load_slot(2)
            for n in range(NX // 2):
                sp.wait_ge(xe_in[n], 16)
            load_slot(3)
            sp.wait_ge(s["downf_done"], B * NF)
            load_slot(4)
            for j in range(NS, NJ):
                sp.wait_ge(s["edn_ready"], j - NS + 1)
                load_slot(j)
            for b in range(B):
                sp.wait_ge(s["final_ready"], b + 1)
                sp.dma_start(out[b].rearrange("(i p) h -> p i h", p=P), x_sb[:, TB * b:TB * b + TB, :]).then_inc(out_done, 16)
            sp.wait_ge(out_done, 16 * B)

        @block.gpsimd
        def _(pool):
            count = [0]

            def link(ins):
                count[0] += 1
                ins.then_inc(s["pool_chain"], 1)
                pool.wait_ge(s["pool_chain"], count[0])

            def band(view, op, base, pattern, mult, fill=1.0):
                return pool.affine_select(out=view, in_=view, compare_op=op, fill=fill, base=base, pattern=pattern, channel_multiplier=mult)

            link(pool.memset(head_rows[:, :, :], 1.0))
            link(band(head_rows[:, :, :], ALU.is_ge, 0, [[-3 * HC, KC], [-3, HC]], 1, 0.0))
            band(head_rows[:, :, :], ALU.is_ge, 2, [[3 * HC, KC], [3, HC]], -1, 0.0).then_inc(s["rows_made"], 1)
            link(pool.memset(ident[:, :], 0.0))
            band(ident[:, :], ALU.not_equal, 0, [[-1, P]], 1).then_inc(s["ident_ready"], 1)
            link(pool.memset(batch_heads[:, :, :, :], 0.0))
            band(batch_heads[:, :, :, :], ALU.not_equal, 0, [[-32, B], [-HC, KC], [-1, HC]], 1).then_inc(s["heads_made"], 1)
            link(pool.memset(row_head[:, :, :], 1.0))
            link(band(row_head[:, :, :], ALU.is_ge, 0, [[-DH * GH, 2], [-DH, GH]], 1, 0.0))
            band(row_head[:, :, :], ALU.is_ge, DH - 1, [[DH * GH, 2], [DH, GH]], -1, 0.0).then_inc(s["heads_made"], 1)
            link(pool.memset(causal[:, :], 0.0))
            band(causal[:, :], ALU.is_ge, 0, [[1, P]], -1, NEG).then_inc(s["masks_made"], 1)
            link(pool.memset(mhalf[:, :], -0.5))

            for b in range(B):
                pool.wait_ge(s["ln1_stats"], b + 1)
                r = slice(TB * b, TB * b + TB)
                link(pool.tensor_scalar(rstd[:, r], mv[:, r, 1], 1e-5, None, ALU.add))
                pool.tensor_tensor(rstd[:, r], rstd[:, r], mhalf[:, 0:TB], ALU.pow).then_inc(s["ln1_rstd"], 1)

            pool.wait_ge(gw_in, 32)
            pool.tensor_tensor(gw[:, KC:2 * KC, :, :], gw[:, KC:2 * KC, :, :], gw[:, 2 * KC:3 * KC, :, :], ALU.add).then_inc(s["gw_summed"], 1)

            def centre_values(b):
                cv = ctx_sb[:, TB * b:TB * b + TB, :].rearrange("p i (h d) -> p i h d", d=DH)
                pool.wait_ge(s["vmean_ready"], b + 1)
                if b >= 2:
                    pool.wait_ge(s["pv_done"], UB * (b - 1))
                for i in range(TB):
                    ins = pool.tensor_tensor(vaug[:, b % 2, i, :, 0:DH], cv[:, i, :, :], vmean[:, i, :].unsqueeze(2).broadcast_to([P, NH, DH]), ALU.subtract)
                ins.then_inc(s["vaug_ready"], 1)

            def weigh_values(b, c):
                pool.wait_ge(s["vaug_ready"], b + 1)
                if b == 0 and c == 0:
                    pool.wait_ge(s["wtnm_ready"], 2)
                if b > 0:
                    pool.wait_ge(s["st_ready"], KC * (b - 1) + c + 1)
                w = wtnm[:, 0, 32 * b + HC * c:32 * b + HC * c + HC].unsqueeze(2).broadcast_to([P, HC, HP])
                pool.tensor_tensor(wv[:, c, :, :], vaug[:, b % 2, 0, HC * c:HC * c + HC, :], w, ALU.mult).then_inc(s["wv_ready"], 1)

            link(pool.memset(ones_b[:, :], 1.0))
            link(pool.memset(before_b[:, :], 1.0))
            link(band(before_b[:, :], ALU.is_gt, 0, [[1, P]], -1, 0.0))
            pool.iota(slot_no[:, :], [[1, CAP]], 0, 0, allow_small_or_imprecise_dtypes=True)
            pool.iota(expert_no[:, :], [[1, NE]], 0, 0, allow_small_or_imprecise_dtypes=True)
            pool.iota(row_no[:, :, 0], [[0, NT]], 0, 1, allow_small_or_imprecise_dtypes=True)
            pool.iota(row_no[:, :, 1], [[P, NT]], 0, 0, allow_small_or_imprecise_dtypes=True)
            link(pool.memset(own_expert[:, :, :], 1.0))
            link(band(own_expert[:, :, :], ALU.is_ge, 0, [[0, NJ], [-CAP, EG]], 1, 0.0))
            band(own_expert[:, :, :], ALU.is_ge, CAP - 1, [[0, NJ], [CAP, EG]], -1, 0.0).then_inc(s["routing_ready"], 1)
            centre_values(0)
            centre_values(1)
            for c in range(KC):
                weigh_values(0, c)
            for m, (raw, hi, lo) in enumerate(weight_parts):
                pool.wait_ge(s["weight_hi"], m + 1)
                pool.tensor_tensor(lo, raw, hi.bitcast(F32), ALU.subtract).then_inc(s["wr_ready" if m == 0 else "wshared_ready"], 1)

            def gather(j):
                if j == 0:
                    pool.wait_ge(s["idx_int"], 1)
                    for b in range(B):
                        pool.wait_ge(rows_out[b], 16)
                    pool.wait_ge(s["pv_done"], NU)
                    pool.wait_ge(s["ht_ready"], NT)
                    pool.wait_ge(s["norm1"], NT)
                    pool.wait_ge(s["x_new"], NT)
                if j >= NX:
                    pool.wait_ge(s["xet_ready"], j - NX + 1)
                    pool.wait_ge(s["wslot_ready"], j - NX + 1)
                pool.indirect_dma_start(xe[:, j % NX, :], None, rows[:, :], bass.IndirectOffsetOnAxis(ap=idx[:, j:j + 1], axis=0)).then_inc(xe_in[j % NX], 16)

            for n in range(LAST + 1):
                k = (n - 5) // 4
                if n >= 5 and (n - 5) % 4 == 0 and k < NT:
                    pool.wait_ge(s["norm1"], k + 1)
                    ins = pool.tensor_tensor(rs[:, k % 2, :], ssq[:, k % 2, :], mhalf[:, :], ALU.pow)
                    ins.then_inc(s["norm_rs"], 1)
                k = tile_at(n, 6)
                if k is not None:
                    pool.wait_ge(s["ln2_stats"], k + 1)
                    link(pool.tensor_scalar(rstd[:, k:k + 1], mv[:, k, 1:2], 1e-5, None, ALU.add))
                    pool.tensor_tensor(rstd[:, k:k + 1], rstd[:, k:k + 1], mhalf[:, 0:1], ALU.pow).then_inc(s["ln2_rstd"], 1)
                    pool.wait_ge(s["ln2_rstd"], k + 1)
                    b, i = divmod(k, TB)
                    if b >= 2:
                        pool.wait_ge(rows_out[b - 2], 16)
                    if k < NT - 1:
                        pool.tensor_scalar(x2w[:, b % 2, i, 0:H], x_sb[:, k, :], mv[:, k, 0:1], rstd[:, k:k + 1], ALU.subtract, ALU.mult).then_inc(s["x2_ready"], 1)
                b, u = divmod(n, UB)
                if b >= 1 and b + 1 < B and u == 3:
                    centre_values(b + 1)
                if b + 1 < B and u in (5, 7):
                    c = (u - 5) // 2
                    weigh_values(b + 1, c)
                bf_ = ffn_at(n, 1)
                if bf_ and bf_[0] < B - 1:
                    b, f = bf_
                    m = NF * b + f
                    w = FCH[f][1]
                    pool.wait_ge(s["hhi_ready"], m + 1)
                    pool.tensor_tensor(h_lo[0:w, m % 3, :], hf[0:w, m % 2, :], h_hi[0:w, m % 3, :].bitcast(F32), ALU.subtract).then_inc(s["hlo_ready"], 1)
            for j in range(NJ):
                gather(j)

        @block.scalar
        def _(act):
            count = [0]

            def link(ins):
                count[0] += 1
                ins.then_inc(s["act_chain"], 1)
                act.wait_ge(s["act_chain"], count[0])

            def build_qbd(b, g):
                c, r = divmod(g, NG // KC)
                if b > 0:
                    act.wait_ge(s["qk_ready"], UB * (b - 1) + NG + g + 1)
                for h in range(GH * r, GH * r + GH):
                    ins = act.activation(qbd[:, c, h, :], qT[:, c, b * S:(b + 1) * S], ACT.Copy, scale=row_head[:, h // GH, h % GH:h % GH + 1])
                ins.then_inc(s["qbd_ready"], 1)

            def weight_hi(m):
                if m == 0:
                    act.wait_ge(wr_in, 32)
                elif m == 1:
                    act.wait_ge(stage_in, 64)
                raw, hi, lo = weight_parts[m]
                act.activation(hi, raw, ACT.Copy).then_inc(s["weight_hi"], 1)

            for n in range(2 * B):
                b = n // 2
                act.wait_ge(s["tposed"], n + 1)
                dst = (ctxT if n % 2 == 0 else qT)[:, :, b * S:(b + 1) * S]
                act.activation(dst, bank[n % 4][:, :].rearrange("p (c t) -> p c t", c=KC), ACT.Copy).then_inc(s["t_evac"], 1)
            act.wait_ge(s["t_evac"], 2)
            act.wait_ge(s["heads_made"], 2)
            build_qbd(0, 0)
            act.wait_ge(s["rows_made"], 1)
            act.activation(arg_r[0:3 * NH, :, :, :].rearrange("p c h s -> p (c h) s"),
                           head_rows[0:3 * NH, :, :].rearrange("p c h -> p (c h)").unsqueeze(2).broadcast_to([3 * NH, NH, S]), ACT.Copy).then_inc(s["selector_ready"], 1)
            act.wait_ge(s["gates_ln_in"], 1)
            act.activation(nm[:, :], g1[:, :], ACT.Exp, scale=-1.0).then_inc(s["gates_e"], 1)
            act.wait_ge(s["gates_e"], 1)
            act.activation(nm[:, :], nm[:, :], ACT.Ln, bias=1.0).then_inc(s["gates_l"], 1)
            for g in range(1, NG):
                build_qbd(0, g)
            act.wait_ge(s["a_ready"], 1)
            act.activation(wfac[:, :], aa[:, 0:P], ACT.Exp, bias=negA0[:, :]).then_inc(s["fac_ready"], 1)
            act.activation(rfac[:, :], mm_[:, P:S], ACT.Exp, scale=-1.0, bias=mm_[:, P - 1:P]).then_inc(s["fac_ready"], 1)
            act.activation(nm[:, :], nm[:, :], ACT.Exp, scale=-1.0).then_inc(s["fac_ready"], 1)
            act.wait_ge(s["fact_ready"], 1)
            act.activation(wtnm[:, 1:3, :], ht_ps[:, P:3 * P].rearrange("p (a t) -> p a t", a=2), ACT.Copy, bias=1e-6).then_inc(s["wtnm_ready"], 1)
            act.activation(wtnm[:, 0, :], ht_ps[:, 0:P], ACT.Copy).then_inc(s["wtnm_ready"], 1)

            def shared_tanh(n):
                b, f = ffn_at(n, 0)
                m = NF * b + f
                w = FCH[f][1]
                act.wait_ge(s["up_ready"], m + 1)
                if m >= 2:
                    act.wait_ge(s["h_ready"], m - 1)
                act.activation(th[0:w, m % 2, :], up_bank(n)[0:w, 0:S], ACT.Tanh, scale=0.5).then_inc(s["th_ready"], 1)

            for n in range(LAST + 1):
                if n < NU:
                    act.wait_ge(s["arg_ready"], n + 1)
                    if n >= 2:
                        act.wait_ge(s["c_ready"], n - 1)
                    act.activation(dd[:, n % 2, :, :], arg_ps[:, :].rearrange("p (h t) -> p h t", h=GH), ACT.Exp).then_inc(s["d_ready"], 1)
                if n < len(weight_parts):
                    weight_hi(n)
                b, g = divmod(n - 5, UB)
                if n >= 5 and b + 1 < B and g < NG:
                    build_qbd(b + 1, g)
                if n >= 4 and n % 4 == 0 and n // 4 - 1 < NT:
                    k = n // 4 - 1
                    act.wait_ge(s["pv_done"], 4 * k + 4)
                    if k >= 2:
                        act.wait_ge(s["ht_ready"], k - 1)
                    act.activation(hT[:, k % 2, :, :], pv_ps[:, :].rearrange("p (g t) -> p g t", g=NG), ACT.Copy).then_inc(s["pv_evac"], 1)
                bf_ = ffn_at(n, 1)
                if bf_:
                    b, f = bf_
                    m = NF * b + f
                    w = FCH[f][1]
                    act.wait_ge(s["h_ready"], m + 1)
                    if m >= 3:
                        act.wait_ge(s["downf_done"], m - 2)
                    act.activation(h_hi[0:w, m % 3, :], hf[0:w, m % 2, :], ACT.Copy).then_inc(s["hhi_ready"], 1)
                if n == NU + 4:
                    shared_tanh(n)
                b = after_batch(n, 4)
                if b is not None:
                    act.wait_ge(s["x2t_ready"], b + 1)
                    if b >= 2:
                        act.wait_ge(s["up_ready"], NF * (b - 1))
                        act.wait_ge(s["logits_ready"], b - 1)
                    act.activation(x2t_hi[:, b % 2, :, :], misc_ps[:, :].rearrange("p (c t) -> p c t", c=KC), ACT.Copy).then_inc(s["x2hi_ready"], 1)
                b = after_batch(n, 6, 4)
                if b is not None:
                    act.wait_ge(s["nmax_ready"], b + 1)
                    for i in range(TB):
                        act.activation(ex[:, i, :], lg[:, i, 0:NE], ACT.Exp, bias=nmax[:, i:i + 1]).then_inc(s["ex_ready"], 1)
                    act.activation(gate[:, TB * b:TB * b + TB], lg[:, :, NE], ACT.Tanh, scale=0.5).then_inc(s["gate_th"], 1)
                b = after_batch(n, 8)
                if b is not None and b < B - 1:
                    act.wait_ge(s["rw_ready"], b + 1)
                    store_rows(act, b)
                if n != NU + 4 and ffn_at(n, 0):
                    shared_tanh(n)
            def evacuate_rows(j):
                act.wait_ge(s["xet_ready"], j + 1)
                act.activation(xeT[:, j % 2, :, :], misc_ps[:, 0:KC * P].rearrange("p (c t) -> p c t", c=KC), ACT.Copy).then_inc(s["xet_evac"], 1)

            evacuate_rows(0)
            for j in range(-1, NJ):
                if j + 1 < NJ:
                    act.wait_ge(s["eup_ready"], j + 2)
                    if j >= 0:
                        act.wait_ge(s["eh_ready"], j + 1)
                    act.activation(eth[:, :], eup_ps[:, 0:F], ACT.Tanh, scale=0.5).then_inc(s["eth_ready"], 1)
                    if j + 2 < NJ:
                        evacuate_rows(j + 2)
                    act.wait_ge(s["back_ready"], j + 2)
                    if j >= 1:
                        act.wait_ge(s["comb_done"], j)
                    act.activation(back[:, (j + 1) % 2, :], back_ps[:, :].bitcast(BF16), ACT.Copy).then_inc(s["back_evac"], 1)
                    act.wait_ge(s["edn_ready"], j + 2)
                    act.wait_ge(s["wslot_ready"], j + 2)
                    if j >= 1:
                        act.wait_ge(s["comb_done"], j)
                    act.activation(y_hi[:, (j + 1) % 2, :], edn_ps[:, 0:H], ACT.Copy, scale=wslot[:, j + 1:j + 2]).then_inc(s["yhi_ready"], 1)

        @block.tensor
        def _(pe):
            pe.wait_ge(s["ident_ready"], 1)
            for n in range(2 * B):
                b = n // 2
                if n % 2 == 0:
                    pe.wait_ge(ctx_in[b], 16)
                else:
                    pe.wait_ge(s["qn_ready"], b + 1)
                if n >= 4:
                    pe.wait_ge(s["t_evac"], n - 3)
                src = ctx_sb if n % 2 == 0 else qn
                for c in range(KC):
                    for i in range(TB):
                        last = pe.transpose(bank[n % 4][:, (TB * c + i) * P:(TB * c + i + 1) * P], src[:, TB * b + i, c * P:(c + 1) * P], ident[:, :])
                last.then_inc(s["tposed"], 1)
            pe.wait_ge(s["gw_summed"], 1)
            for b in range(B):
                pe.wait_ge(s["t_evac"], 2 * b + 2)
                for gi in range(2):
                    for k in range(2 * KC):
                        src = qT if k < KC else ctxT
                        last = pe.matmul(misc_ps[32 * b:32 * b + 32, gi * S:(gi + 1) * S], gw[:, k, gi, :], src[:, k % KC, b * S:(b + 1) * S],
                                         start=(k == 0), stop=(k == 2 * KC - 1))
            last.then_inc(s["gates_ready"], 1)
            def keys_queries(n):
                b, i, g, c, r = unit(n)
                if i == 0:
                    pe.wait_ge(s["qbd_ready"], NG * b + g + 1)
                if n >= 2:
                    pe.wait_ge(s["c_ready"], n - 1)
                pe.matmul(qk_ps[n % 2][:, :], ctxT[:, c, tok(b, i)], qbd[:, c, GH * r:GH * r + GH, i * P:(i + 1) * P],
                          start=True, stop=True).then_inc(s["qk_ready"], 1)

            keys_queries(0)
            keys_queries(1)
            pe.wait_ge(s["fac_ready"], 3)
            for a, src in enumerate((wfac[:, :], nm[:, 0:P], nm[:, P:S])):
                last = pe.transpose(ht_ps[:, a * P:(a + 1) * P], src, ident[:, :])
            last.then_inc(s["fact_ready"], 1)
            pe.wait_ge(s["selector_ready"], 1)
            pe.wait_ge(s["masks_made"], 1)
            pe.wait_ge(s["identb_ready"], 1)
            pe.wait_ge(s["vpads_ready"], 1)

            def values(n):
                b, i, g, c, r = unit(n)
                pe.wait_ge(s["c_ready"], n + 1)
                if g == 0 and n > 0:
                    pe.wait_ge(s["pv_evac"], n // 4)
                if g == 0:
                    pe.wait_ge(s["vaug_ready"], b + 1)
                o = pv_ps[:, g * P:(g + 1) * P]
                if i == 1:
                    pe.wait_ge(s["state_ready"], KC * b + c + 1)
                    pe.matmul(o, state[:, c, GH * r:GH * r + GH, :].rearrange("p h e -> p (h e)"), qr[:, c, :], start=True, stop=False, skip_group_check=True)
                for h in range(GH):
                    last = pe.matmul(o[32 * h:32 * h + 32, :], vaug[:, b % 2, i, GH * g + h, :], cc[:, n % 2, h, :],
                                     start=(i == 0), stop=True, skip_group_check=True)
                last.then_inc(s["pv_done"], 1)

            def shared_up(n):
                b, f = ffn_at(n, 0)
                m = NF * b + f
                f0, w = FCH[f]
                if m == 0:
                    pe.wait_ge(s["wshared_ready"], len(weight_parts) - 1)
                if f == 0:
                    pe.wait_ge(s["x2lo_ready"], b + 1)
                pe.wait_ge(s["state_ready"], sum(k < NU and k % UB in (3, 4) for k in range(n + 1)))
                wait_up_used(pe, up_bank(n), n)
                if up_bank(n) is ht_ps:
                    pe.wait_ge(s["norm1"], (n - 5) // 4 + 1)
                if f == NF - 1:
                    for k in range(KC):
                        for q, (ws, xs) in enumerate(((wut_hi, x2t_hi), (wut_hi, x2t_lo), (wut_lo, x2t_hi))):
                            last = pe.matmul(up_bank(n)[0:2 * w, 0:S], ws[:, k, :], xs[:, b % 2, k, :], start=(k == 0 and q == 0), stop=(k == KC - 1 and q == 2))
                else:
                    for gu in range(2):
                        for k in range(KC):
                            for q, (ws, xs) in enumerate(((wu_hi, x2t_hi), (wu_hi, x2t_lo), (wu_lo, x2t_hi))):
                                last = pe.matmul(up_bank(n)[:, gu * S:(gu + 1) * S], ws[:, k, gu, f0:f0 + w], xs[:, b % 2, k, :],
                                                 start=(k == 0 and q == 0), stop=(k == KC - 1 and q == 2))
                last.then_inc(s["up_ready"], 1)

            def shared_down(n):
                b, f = down_steps[n]
                m = NF * b + f
                w = FCH[f][1]
                wait_low(pe, m)
                if f == 0 and b > 0:
                    pe.wait_ge(s["base_ready"], b)
                for i in range(TB):
                    for q, (hs, ws) in enumerate(((h_hi, wd_hi), (h_hi, wd_lo), (h_lo, wd_hi))):
                        last = pe.matmul(down_ps[:, i * H:(i + 1) * H], hs[0:w, m % 3, i * P:(i + 1) * P], ws[0:w, f, :],
                                         start=(f == 0 and i == 0 and q == 0), stop=(f == NF - 1 and q == 2), skip_group_check=True)
                last.then_inc(s["downf_done"], 1)

            def rows_T(j):
                pe.wait_ge(xe_in[j % NX], 16 * (j // NX + 1))
                if j == 0:
                    pe.wait_ge(s["idx_added"], B)
                else:
                    pe.wait_ge(s["xet_evac"], j)
                xv = xe[:, j % NX, 0:H].rearrange("p (m k) -> p k m", k=KC)
                for k in range(KC):
                    last = pe.transpose(misc_ps[:, k * P:(k + 1) * P], xv[:, k, :], ident[:, :])
                last.then_inc(s["xet_ready"], 1)

            def back_T(j):
                if j == 0:
                    pe.wait_ge(s["h_ready"], NF * B)
                else:
                    pe.wait_ge(s["back_evac"], j)
                for t in range(NT):
                    pk = pick[:, t, P * j:P * (j + 1)]
                    last = pe.transpose(back_ps[:, :].bitcast(BF16)[:, t * P:(t + 1) * P], pk, ident_b[:, :])
                last.then_inc(s["back_ready"], 1)

            def expert_up(j):
                pe.wait_ge(s["xet_evac"], j + 1)
                pe.wait_ge(slot_in[j % NS], 48 * (j // NS + 1))
                if j == 0:
                    pe.wait_ge(s["norm1"], NT)
                else:
                    pe.wait_ge(s["eh_ready"], j)
                for k in range(KC):
                    for e in range(EG):
                        last = pe.matmul(eup_ps[32 * e:32 * e + 32, 0:2 * F], xeT[:, j % 2, k, 32 * e:32 * e + 32], we_up[j % NS][:, e, :, k, :],
                                         start=(k == 0), stop=(k == KC - 1), skip_group_check=True)
                last.then_inc(s["eup_ready"], 1)

            def hidden_T(j):
                pe.wait_ge(s["eh_ready"], j + 1)
                pe.wait_ge(s["xet_evac"], min(j + 2, NJ))
                ev = eh[:, :].rearrange("p (m k) -> p k m", k=2)
                for k in range(2):
                    last = pe.transpose(misc_ps[0:FK, (KC + k) * P:(KC + k + 1) * P], ev[:, k, :], ident[:, :])
                last.then_inc(s["eht_ready"], 1)

            def expert_down(j):
                pe.wait_ge(s["eht_evac"], j + 1)
                if j == 0:
                    pe.wait_ge(s["base_ready"], B)
                else:
                    pe.wait_ge(s["ylo_ready"], j)
                for k in range(2):
                    for e in range(EG):
                        last = pe.matmul(edn_ps[32 * e:32 * e + 32, 0:H], ehT[:, k, 32 * e:32 * e + 32], we_dn[j % NS][0:FK, e, k, :],
                                         start=(k == 0), stop=(k == 1), skip_group_check=True)
                last.then_inc(s["edn_ready"], 1)

            def combine(j, tiles):
                pe.wait_ge(s["back_evac"], j + 1)
                pe.wait_ge(s["ylo_ready"], j + 1)
                if j == 0:
                    pe.wait_ge(s["pv_evac"], NT)
                for t in tiles:
                    for q, ys in enumerate((y_hi, y_lo)):
                        last = pe.matmul(acc_ps[t // 2][:, (t % 2) * H:(t % 2 + 1) * H], back[:, j % 2, t * P:(t + 1) * P], ys[:, j % 2, :],
                                         start=(j == 0 and q == 0 and t % 2 == 0), stop=(j == NJ - 1 and q == 1), skip_group_check=True)
                    if j == NJ - 1 and t % 2 == 1:
                        last.then_inc(s["acc_ready"], 1)
                if j < NJ - 1 and tiles[-1] == NT - 1:
                    last.then_inc(s["comb_done"], 1)

            for n in range(LAST + 1):
                if n < NU:
                    b, i, g, c, r = unit(n)
                    if i == 0 and r == 0:
                        pe.wait_ge(argl_in[b], 16)
                        if c == 0 or b > 0:
                            pe.wait_ge(argr_in[c], 48 * (b + (c == 0)))
                    if n >= 1:
                        pe.wait_ge(s["d_ready"], n)
                    pe.matmul(arg_ps[:, :], arg_l[:, b, i * P:(i + 1) * P], arg_r[:, c, GH * r:GH * r + GH, i * P:(i + 1) * P], start=True, stop=False)
                    pe.matmul(arg_ps[:, :], ident_b[:, :], causal[:, :].unsqueeze(1).broadcast_to([P, GH, P]), start=False, stop=True).then_inc(s["arg_ready"], 1)
                    if n >= 2:
                        keys_queries(n)
                if 1 <= n <= NU:
                    values(n - 1)
                if n >= 5 and (n - 5) % 4 == 0 and (n - 5) // 4 < NT:
                    k = (n - 5) // 4
                    pe.wait_ge(s["pv_evac"], k + 1)
                    if k >= 1:
                        pe.wait_ge(s["norm1"], k)
                    wait_up_used(pe, ht_ps, n)
                    for g in range(NG):
                        last = pe.transpose(ht_ps[:, g * P:(g + 1) * P], hT[:, k % 2, g, :], ident[:, :])
                    last.then_inc(s["ht_ready"], 1)
                b, u = divmod(n, UB)
                if b < B and u in (3, 4):
                    c = u - 3
                    pe.wait_ge(s["wv_ready"], KC * b + c + 1)
                    if b == 0 and c == 0:
                        pe.wait_ge(s["masks_ready"], 1)
                    if b > 0 or c > 0:
                        pe.wait_ge(s["state_ready"], KC * b + c)
                    wait_up_used(pe, up_ps, n)
                    pe.matmul(up_ps[:, 0:HC * HP], ctx_sb[:, TB * b, c * P:(c + 1) * P], wv[:, c, :, :].rearrange("p h e -> p (h e)"), start=True, stop=True)
                    pe.matmul(up_ps[:, HC * HP:HC * HP + P], headsel[:, b, c, :], rfac[:, :], start=True, stop=True, skip_group_check=True).then_inc(s["st_ready"], 1)
                if n == NU + 4:
                    shared_up(n)
                b = after_batch(n, 4)
                if b is not None:
                    pe.wait_ge(s["x2_ready"], min(TB * (b + 1), NT - 1))
                    if b == B - 1:
                        pe.wait_ge(s["x2_last"], 1)
                    if b == 0:
                        pe.wait_ge(s["a_ready"], 1)
                    else:
                        pe.wait_ge(s["idx_added"], b)
                    for c in range(KC):
                        for i in range(TB):
                            last = pe.transpose(misc_ps[:, (TB * c + i) * P:(TB * c + i + 1) * P], x2w[:, b % 2, i, c * P:(c + 1) * P], ident[:, :])
                    last.then_inc(s["x2t_ready"], 1)
                if n <= NU + 4 and n in down_steps:
                    shared_down(n)
                b = after_batch(n, 5, 4)
                if b is not None:
                    pe.wait_ge(s["x2lo_ready"], b + 1)
                    if b == 0:
                        pe.wait_ge(s["wr_ready"], 1)
                    for i in range(TB):
                        for k in range(KC):
                            for m, (xs, ws) in enumerate(((x2t_hi, wr_hi), (x2t_hi, wr_lo), (x2t_lo, wr_hi))):
                                last = pe.matmul(misc_ps[:, RC * i:RC * i + RC], xs[:, b % 2, k, i * P:(i + 1) * P], ws[:, k, :],
                                                 start=(k == 0 and m == 0), stop=(k == KC - 1 and m == 2))
                    last.then_inc(s["logits_ready"], 1)
                if n > NU + 4 and ffn_at(n, 0):
                    shared_up(n)
                b = after_batch(n, 7)
                if b is not None:
                    pe.wait_ge(s["sel_ready"], b + 1)
                    if b == 0:
                        pe.wait_ge(s["routing_ready"], 1)
                    for i in range(TB):
                        pe.matmul(misc_ps[:, NE * i:NE * i + NE], ones_b[:, :], sofar[:, TB * b + i, :], start=True, stop=False)
                        last = pe.matmul(misc_ps[:, NE * i:NE * i + NE], before_b[:, :], sel_b[:, i, :], start=False, stop=True)
                    last.then_inc(s["excl_ready"], 1)
                if n > NU + 4 and n in down_steps:
                    shared_down(n)
                b = index_steps.get(n)
                if b is not None:
                    pe.wait_ge(s["pick_ready"], TB * (b + 1))
                    for j in range(NJ):
                        for i in range(TB):
                            pk = pick[:, TB * b + i, P * j:P * (j + 1)]
                            last = pe.matmul(misc_ps[:, 2 * j:2 * j + 2], pk, row_no[:, TB * b + i, :], start=(i == 0), stop=(i == TB - 1))
                    last.then_inc(s["idx_ready"], 1)
                if n < NU + 4 and ffn_at(n, 0):
                    shared_up(n)
                if n == LAST - 2:
                    rows_T(0)
                    back_T(0)
                if n == LAST - 1:
                    expert_up(0)

            first = range(0, 5)
            for j in range(-1, NJ):
                if j + 1 < NJ:
                    if j >= 0:
                        expert_up(j + 1)
                    if j + 2 < NJ:
                        rows_T(j + 2)
                    if j >= 0:
                        back_T(j + 1)
                if j >= 0:
                    combine(j, first)
                if j + 1 < NJ:
                    hidden_T(j + 1)
                if j >= 0:
                    combine(j, range(first.stop, NT))
                if j + 1 < NJ:
                    expert_down(j + 1)

        @block.vector
        def _(dve):
            count = [0]

            def link(ins):
                count[0] += 1
                ins.then_inc(s["dve_chain"], 1)
                dve.wait_ge(s["dve_chain"], count[0])

            def head_values(b):
                dve.wait_ge(ctx_in[b], 16)
                cv = ctx_sb[:, TB * b:TB * b + TB, :].rearrange("p i (h d) -> p i h d", d=DH)
                if b > 0:
                    dve.wait_ge(s["vaug_ready"], b)
                link(dve.tensor_reduce(vmean[:, :, :], cv, AX.X, ALU.add))
                dve.tensor_scalar(vmean[:, :, :], vmean[:, :, :], 1.0 / DH, None, ALU.mult).then_inc(s["vmean_ready"], 1)

            dve.memset(gw[:, :, :, :], 0.0).then_inc(s["pads_zero"], 1)
            dve.memset(bias[:, :], 0.0).then_inc(s["pads_zero"], 1)
            dve.memset(wr_raw[:, :, :], 0.0).then_inc(s["pads_zero"], 1)
            dve.memset(arg_l[:, :, :], -1.0).then_inc(s["minus_ready"], 1)
            dve.memset(vaug[:, :, :, :, DH:DH + 1], 1.0)
            dve.memset(vaug[:, :, :, :, DH + 1:HP], 0.0).then_inc(s["vpads_ready"], 1)
            link(dve.memset(sofar[:, 0, :], 0.0))
            link(dve.memset(idxf[:, :, :], 0.0))
            link(dve.memset(aa[:, :], 1.0))
            for step in range(B + 1):
                if step < B:
                    b = step
                    dve.wait_ge(x_in[b], 16)
                    for t in range(TB * b, TB * b + TB):
                        link(dve.bn_stats(stats[:, t, :], x_sb[:, t, :]))
                        ins = dve.bn_aggr(mv[:, t, :], stats[:, t, :])
                    ins.then_inc(s["ln1_stats"], 1)
                if step > 0:
                    b = step - 1
                    dve.wait_ge(s["ln1_rstd"], b + 1)
                    for t in range(TB * b, TB * b + TB):
                        ins = dve.tensor_scalar(qn[:, t, :], x_sb[:, t, :], mv[:, t, 0:1], rstd[:, t:t + 1], ALU.subtract, ALU.mult)
                    ins.then_inc(s["qn_ready"], 1)
            dve.wait_ge(s["ident_ready"], 1)
            dve.tensor_copy(ident_b[:, :], ident[:, :]).then_inc(s["identb_ready"], 1)
            dve.wait_ge(s["heads_made"], 2)
            dve.tensor_copy(headsel[:, :, :, :].rearrange("p b c (h d) -> p (b c h) d", d=DH),
                            batch_heads[:, :, :, :].rearrange("p b c h -> p (b c h)").unsqueeze(2).broadcast_to([P, B * NH, DH]))
            link(dve.tensor_scalar(blockmask[:, :, :], row_head[:, :, :].rearrange("p a h -> p (a h)").unsqueeze(2).broadcast_to([P, HC, HP]),
                                   float(DH) ** -0.5, None, ALU.mult))
            dve.memset(th[:, 0, 0:1], 0.0).then_inc(s["masks_ready"], 1)
            head_values(0)
            head_values(1)
            dve.wait_ge(s["gates_ready"], 1)
            dve.wait_ge(bias_in, 32 * B)
            dve.tensor_scalar(ig[:, :], misc_ps[:, 0:S], bias[:, 0:1], None, ALU.add)
            link(dve.tensor_scalar(g2[:, :], misc_ps[:, S:2 * S], bias[:, 1:2], None, ALU.add))
            dve.scalar_tensor_tensor(g1[:, :], g2[:, :], -1.0, g2[:, :], ALU.mult, ALU.max).then_inc(s["gates_ln_in"], 1)
            link(dve.tensor_scalar(cum[:, :], g2[:, :], 0.0, None, ALU.min))
            dve.wait_ge(s["gates_l"], 1)
            link(dve.tensor_tensor(g2[:, :], cum[:, :], nm[:, :], ALU.subtract))
            link(dve.tensor_tensor_scan(cum[:, :], aa[:, :], g2[:, :], 0.0, ALU.mult, ALU.add))
            link(dve.tensor_tensor(aa[:, :], ig[:, :], cum[:, :], ALU.subtract))
            link(dve.tensor_tensor_scan(mm_[:, :], aa[:, :], aa[:, :], -3.0e38, ALU.max, ALU.max))
            for src, parts in ((aa, a_part), (mm_, m_part)):
                link(dve.tensor_copy(parts[:, 0, :], src[:, :]))
                link(dve.tensor_tensor(g1[:, :], src[:, :], parts[:, 0, :], ALU.subtract))
                link(dve.tensor_copy(parts[:, 1, :], g1[:, :]))
                link(dve.tensor_tensor(g2[:, :], g1[:, :], parts[:, 1, :], ALU.subtract))
                dve.tensor_copy(parts[:, 2, :], g2[:, :]).then_inc(s["parts_ready"], 1)
            link(dve.tensor_scalar(negA0[:, :], mm_[:, P - 1:P], -1.0, None, ALU.mult))
            dve.tensor_tensor(nm[:, :], cum[:, :], mm_[:, :], ALU.add).then_inc(s["a_ready"], 1)

            def slots_taken(b):
                dve.wait_ge(s["excl_ready"], b + 1)
                link(dve.tensor_scalar(vt[:, :, :].rearrange("p i e -> p (i e)"), misc_ps[:, 0:TB * NE], 64.0, 128.0, ALU.min, ALU.add))
                link(dve.scalar_tensor_tensor(vb[:, :, :].rearrange("p i e -> p (i e)"), sel[:, :, :].rearrange("p i e -> p (i e)"), -128.0,
                                              vt[:, :, :].rearrange("p i e -> p (i e)"), ALU.mult, ALU.add))

            def pick_slots(b, i):
                return dve.tensor_tensor(pick[:, TB * b + i, :].rearrange("p (e c) -> p e c", c=CAP), vb[:, i, :].unsqueeze(2).broadcast_to([P, NE, CAP]),
                                         slot_no[:, :].unsqueeze(1).broadcast_to([P, NE, CAP]), ALU.is_equal)

            def shared_hidden(n):
                b, f = ffn_at(n, 0)
                m = NF * b + f
                w = FCH[f][1]
                ps = up_bank(n)
                dve.wait_ge(s["th_ready"], m + 1)
                link(dve.scalar_tensor_tensor(s1[0:w, m % 2, :], th[0:w, m % 2, :], 1.0, ps[0:w, 0:S], ALU.add, ALU.mult))
                if m >= 2:
                    wait_low(dve, m - 2)
                up = ps[w:2 * w, 0:S] if f == NF - 1 else ps[:, S:2 * S]
                dve.scalar_tensor_tensor(hf[0:w, m % 2, :], s1[0:w, m % 2, :], 0.5, up, ALU.mult, ALU.mult).then_inc(s["h_ready"], 1)

            def expert_hidden(j):
                dve.wait_ge(xe_in[j % NX], 16 * (j // NX + 1))
                link(dve.tensor_tensor(w4[:, j, :], xe[:, j % NX, H + EG * j:H + EG * j + EG], own_expert[:, j, :], ALU.mult))
                dve.tensor_reduce(wslot[:, j:j + 1], w4[:, j, :], AX.X, ALU.add).then_inc(s["wslot_ready"], 1)
                dve.wait_ge(s["eth_ready"], j + 1)
                link(dve.scalar_tensor_tensor(es1[:, :], eth[:, :], 1.0, eup_ps[:, 0:F], ALU.add, ALU.mult))
                if j > 0:
                    dve.wait_ge(s["eht_ready"], j)
                dve.scalar_tensor_tensor(eh[:, :], es1[:, :], 0.5, eup_ps[:, F:2 * F], ALU.mult, ALU.mult).then_inc(s["eh_ready"], 1)

            for n in range(LAST + 1):
                hidden_first = NU < n <= NU + 4
                if hidden_first and ffn_at(n, 0):
                    shared_hidden(n)
                if n < NU:
                    dve.wait_ge(s["d_ready"], n + 1)
                    dve.wait_ge(s["qk_ready"], n + 1)
                    if n >= 2:
                        dve.wait_ge(s["pv_done"], n - 1)
                    dve.scalar_tensor_tensor(cc[:, n % 2, :, :].rearrange("p h t -> p (h t)"), qk_ps[n % 2][:, :], float(DH) ** -0.5,
                                             dd[:, n % 2, :, :].rearrange("p h t -> p (h t)"), ALU.mult, ALU.mult).then_inc(s["c_ready"], 1)
                b, u = divmod(n, UB)
                if b < B and u in (3, 4):
                    c = u - 3
                    dve.wait_ge(s["st_ready"], KC * b + c + 1)
                    if b > 0:
                        dve.wait_ge(s["pv_done"], UB * (b - 1) + NG + (NG // KC) * (c + 1))
                    dve.tensor_tensor(state[:, c, :, :].rearrange("p h e -> p (h e)"), up_ps[:, 0:HC * HP], blockmask[:, :, :].rearrange("p h e -> p (h e)"), ALU.mult)
                    dve.tensor_tensor(qr[:, c, :], up_ps[:, HC * HP:HC * HP + P], qT[:, c, tok(b, 1)], ALU.mult).then_inc(s["state_ready"], 1)
                if b >= 1 and b + 1 < B and u == 3:
                    head_values(b + 1)
                k = (n - 5) // 4
                if n >= 5 and (n - 5) % 4 == 0 and k < NT:
                    b, i = divmod(k, TB)
                    dve.wait_ge(s["ht_ready"], k + 1)
                    if k == 0:
                        dve.wait_ge(s["wtnm_ready"], 2)
                    d, v, q = den[:, k % 2, :], inv[:, k % 2, :], hv[:, k % 2, :, :]
                    bound = wtnm[:, 1 + i, 32 * b:32 * b + NH]
                    link(dve.scalar_tensor_tensor(d, ht3[:, :, DH], 1e-6, bound, ALU.subtract, ALU.max, reverse0=True))
                    link(dve.scalar_tensor_tensor(d, ht3[:, :, DH], 1e-6, d, ALU.add, ALU.max))
                    link(dve.reciprocal(v, d))
                    link(dve.tensor_tensor(q, ht3[:, :, 0:DH], v.unsqueeze(2).broadcast_to([P, NH, DH]), ALU.mult))
                    link(dve.tensor_tensor(yy[:, :, :], q, q, ALU.mult))
                    link(dve.tensor_reduce(ssq[:, k % 2, :], yy[:, :, :], AX.X, ALU.add))
                    dve.tensor_scalar(ssq[:, k % 2, :], ssq[:, k % 2, :], 1.0 / DH, 1e-6, ALU.mult, ALU.add).then_inc(s["norm1"], 1)
                    if k == 0:
                        dve.wait_ge(ln_in, 16)
                    link(dve.tensor_tensor(q, q, ln_bc[:, :].rearrange("p (h d) -> p h d", d=DH), ALU.mult))
                if n == NU + 1:
                    pick_slots(B - 2, 1).then_inc(s["pick_ready"], 1)
                k = tile_at(n, 6)
                if k is not None:
                    dve.wait_ge(s["norm_rs"], k + 1)
                    link(dve.tensor_tensor(yy[:, :, :], hv[:, k % 2, :, :],
                                           rs[:, k % 2, :].unsqueeze(2).broadcast_to([P, NH, DH]), ALU.mult))
                    dve.tensor_tensor(x_sb[:, k, :], x_sb[:, k, :], yy[:, :, :].rearrange("p h d -> p (h d)"), ALU.add).then_inc(s["x_new"], 1)
                    dve.wait_ge(s["x_new"], k + 1)
                    link(dve.bn_stats(stats[:, k, :], x_sb[:, k, :]))
                    dve.bn_aggr(mv[:, k, :], stats[:, k, :]).then_inc(s["ln2_stats"], 1)
                if tile_at(n, 7) == NT - 1:
                    dve.wait_ge(s["ln2_rstd"], NT)
                    dve.tensor_scalar(x2w[:, (B - 1) % 2, TB - 1, 0:H], x_sb[:, NT - 1, :], mv[:, NT - 1, 0:1], rstd[:, NT - 1:NT], ALU.subtract, ALU.mult).then_inc(s["x2_last"], 1)
                b = after_batch(n, 4)
                if b is not None:
                    dve.wait_ge(s["x2hi_ready"], b + 1)
                    dve.tensor_tensor(x2t_lo[:, b % 2, :, :].rearrange("p c t -> p (c t)"), misc_ps[:, :],
                                      x2t_hi[:, b % 2, :, :].rearrange("p c t -> p (c t)").bitcast(F32), ALU.subtract).then_inc(s["x2lo_ready"], 1)
                b = after_batch(n, 5, 4)
                if b is not None:
                    dve.wait_ge(s["logits_ready"], b + 1)
                    if b == 0:
                        dve.wait_ge(s["routing_ready"], 1)
                    link(dve.tensor_copy(lg[:, :, :].rearrange("p i c -> p (i c)"), misc_ps[:, 0:TB * RC]))
                    for i in range(TB):
                        ins = dve.max(m8[:, i, :], lg[:, i, 0:NE])
                    link(ins)
                    for i in range(TB):
                        ins = dve.max_index(i8[:, i, :], m8[:, i, :], lg[:, i, 0:NE])
                    link(ins)
                    dve.tensor_scalar(nmax[:, :], m8[:, :, 0], -1.0, None, ALU.mult).then_inc(s["nmax_ready"], 1)
                    link(dve.tensor_copy(i8f[:, :, :], i8[:, :, :]))
                b = after_batch(n, 7, 5)
                if b is not None:
                    dve.wait_ge(s["ex_ready"], TB * (b + 1))
                    for i in range(TB):
                        ins = dve.scalar_tensor_tensor(ex[:, i, :], ex[:, i, :], 1.0, sel[:, i, :], ALU.mult, ALU.mult, accum_out=ssum[:, i:i + 1])
                    link(ins)
                    link(dve.reciprocal(rsum[:, :], ssum[:, :]))
                    for i in range(TB):
                        ins = dve.tensor_scalar(x2w[:, b % 2, i, H:XW], ex[:, i, :], rsum[:, i:i + 1], None, ALU.mult)
                    ins.then_inc(s["rw_ready"], 1)
                    dve.wait_ge(s["gate_th"], b + 1)
                    link(dve.tensor_scalar(gate[:, TB * b:TB * b + TB], gate[:, TB * b:TB * b + TB], 0.5, 0.5, ALU.mult, ALU.add))
                b = after_batch(n, 7)
                if b is not None and b < B - 1:
                    slots_taken(b)
                    pick_slots(b, 0).then_inc(s["pick_ready"], 1)
                b = added_steps.get(n)
                if b is not None:
                    dve.wait_ge(s["idx_ready"], b + 1)
                    dve.tensor_tensor(idxf[:, :, :].rearrange("p j a -> p (j a)"), misc_ps[:, 0:2 * NJ], idxf[:, :, :].rearrange("p j a -> p (j a)"), ALU.add).then_inc(s["idx_added"], 1)
                    if b == B - 1:
                        dve.wait_ge(s["idx_added"], B)
                        dve.tensor_tensor(idx[:, :], idxf[:, :, 0], idxf[:, :, 1], ALU.add).then_inc(s["idx_int"], 1)
                b = after_batch(n, 6, 4)
                if b is not None:
                    for i in range(TB):
                        ins = dve.tensor_tensor(eq4[:, i, :, :], expert_no[:, :].unsqueeze(2).broadcast_to([P, NE, TOPK]),
                                                i8f[:, i, 0:TOPK].unsqueeze(1).broadcast_to([P, NE, TOPK]), ALU.is_equal)
                    link(ins)
                    link(dve.tensor_reduce(sel[:, :, :].rearrange("p i e -> p (i e)"), eq4[:, :, :, :].rearrange("p i e k -> p (i e) k"), AX.X, ALU.add))
                    dve.tensor_copy(sel_b[:, :, :], sel[:, :, :])
                    for t in range(TB * b, TB * b + TB):
                        ins = dve.tensor_tensor(sofar[:, t + 1, :], sofar[:, t, :], sel[:, t % TB, :], ALU.add)
                        if t % TB < TB - 1:
                            link(ins)
                    ins.then_inc(s["sel_ready"], 1)
                    dve.wait_ge(s["sel_ready"], b + 1)
                bf_ = ffn_at(n, 1)
                if bf_ and bf_[0] == B - 1:
                    m = NF * bf_[0] + bf_[1]
                    w = FCH[bf_[1]][1]
                    dve.wait_ge(s["hhi_ready"], m + 1)
                    dve.tensor_tensor(h_lo[0:w, m % 3, :], hf[0:w, m % 2, :], h_hi[0:w, m % 3, :].bitcast(F32), ALU.subtract).then_inc(s["hlo_last"], 1)
                if not hidden_first and ffn_at(n, 0):
                    shared_hidden(n)
                if n == LAST:
                    expert_hidden(0)
                bf_ = down_steps.get(n)
                if bf_ and bf_[1] == NF - 1:
                    b = bf_[0]
                    dve.wait_ge(s["downf_done"], NF * (b + 1))
                    for i in range(TB):
                        t = TB * b + i
                        ins = dve.scalar_tensor_tensor(x_sb[:, t, :], down_ps[:, i * H:(i + 1) * H], gate[:, t:t + 1], x_sb[:, t, :], ALU.mult, ALU.add)
                    ins.then_inc(s["base_ready"], 1)
                b = after_batch(n, 7)
                if b is not None and b < B - 2:
                    pick_slots(b, 1).then_inc(s["pick_ready"], 1)
                if n == NU + 7:
                    slots_taken(B - 1)
                    for i in range(TB):
                        pick_slots(B - 1, i).then_inc(s["pick_ready"], 1)

            for j in range(NJ):
                if j > 0:
                    expert_hidden(j)
                dve.wait_ge(s["eht_ready"], j + 1)
                if j > 0:
                    dve.wait_ge(s["edn_ready"], j)
                dve.tensor_copy(ehT[:, :, :].rearrange("p k t -> p (k t)"), misc_ps[0:FK, KC * P:(KC + 2) * P]).then_inc(s["eht_evac"], 1)
                dve.wait_ge(s["yhi_ready"], j + 1)
                dve.scalar_tensor_tensor(y_lo[:, j % 2, :], edn_ps[:, 0:H], wslot[:, j:j + 1], y_hi[:, j % 2, :].bitcast(F32), ALU.mult, ALU.subtract).then_inc(s["ylo_ready"], 1)
            for q in range(4):
                dve.wait_ge(s["acc_ready"], q + 1)
                xv = x_sb[:, TB * q:TB * q + TB, :].rearrange("p i h -> p (i h)")
                dve.tensor_tensor(xv, acc_ps[q][:, :], xv, ALU.add).then_inc(s["final_ready"], 1)


_INS = ['x', 'ctx_2048', 'L0_xattn_Wi', 'L0_xattn_bi', 'L0_xattn_Wf', 'L0_xattn_bf', 'L0_xattn_ln_scale', 'L0_ffn_Wr', 'L0_ffn_Wg',
        'L0_ffn_Wu', 'L0_ffn_Wd', 'L0_ffn_Wsg', 'L0_ffn_Wsu', 'L0_ffn_Wsd', 'L0_ffn_Wse']
_OUTS = [((4, 256, 256), 'float32')]


def kernel(**inputs):
    import numpy as _np
    import concourse.bacc as _bacc
    from concourse import mybir as _mybir
    from concourse.bass_utils import run_bass_kernel_spmd as _run

    nc = _bacc.Bacc("TRN2", target_bir_lowering=False, num_devices=1)
    arrays, args = {}, []
    for name in _INS:
        a = _np.ascontiguousarray(inputs[name])
        arrays[f"in_{name}_dram"] = a
        args.append(nc.dram_tensor(f"in_{name}_dram", a.shape, _mybir.dt.from_np(a.dtype), kind="ExternalInput").ap())
    for i, (shape, dtype) in enumerate(_OUTS):
        dt = _mybir.dt.from_np(_np.dtype(dtype))
        args.append(nc.dram_tensor(f"out_{i}_dram", shape, dt, kind="ExternalOutput").ap())
    xattn_moe_kernel(nc, *args)
    r = _run(nc, [arrays], core_ids=[0])
    got = tuple(r.results[0][f"out_{i}_dram"] for i in range(len(_OUTS)))
    return got[0]
```
